# Optimizing a Trainium2 kernel written in Bass

```python
import numpy as np
import jax
import jax.numpy as jnp

def _softmax(x, axis=-1):
    return jax.nn.softmax(x, axis=axis)

def _gelu(x):
    return jax.nn.gelu(x, approximate=True)

def _silu(x):
    return jax.nn.silu(x)

def _sigmoid(x):
    return jax.nn.sigmoid(x)

def _layernorm(x, axis=-1, eps=1e-05):
    m = jnp.mean(x, axis=axis, keepdims=True)
    v = jnp.var(x, axis=axis, keepdims=True)
    return (x - m) / jnp.sqrt(v + eps)

def _scatter_add(tgt, idx, src, axis=0):
    return tgt.at[idx].add(src)

def _segment_sum(src, seg, n):
    return jax.ops.segment_sum(src, seg, n)
kernel_name = 'mk_flamingo_gated_d2_seqx_r8_7ef913'

def setup_inputs(seed: int=0):
    np.random.seed(seed)
    _w = jnp.asarray

    def _rec_inputs():
        import jax
        import jax.numpy as jnp
        _rk = jax.random.key(seed)
        x = -0.0003929 + 0.9999 * jax.random.normal(jax.random.fold_in(_rk, 1), (8, 256, 128), jnp.float32)
        _lenS = 256 - jax.random.randint(jax.random.fold_in(_rk, 7), (8,), 0, max(1, 256 // 4) + 1, jnp.int32)
        _lenS2 = 512 - jax.random.randint(jax.random.fold_in(_rk, 8), (8,), 0, max(1, 512 // 4) + 1, jnp.int32)
        _ctx_768P = jax.random.normal(jax.random.fold_in(_rk, 11), (8, 16, 96), jnp.float32)
        _ctx_768c = jax.random.dirichlet(jax.random.fold_in(_rk, 511), 0.3 * jnp.ones((16,), jnp.float32), (8, 512))
        _ctx_768t = jnp.einsum('bsk,bkd->bsd', _ctx_768c, _ctx_768P)
        _ctx_768t = _ctx_768t * jax.lax.rsqrt(jnp.mean(jnp.square(_ctx_768t)) + 1e-12) * 0.953939
        ctx_768 = 2.09791e-05 + 1.00001 * (_ctx_768t + 0.3 * jax.random.normal(jax.random.fold_in(_rk, 611), (8, 512, 96), jnp.float32))
        _g = jax.random.normal(jax.random.fold_in(_rk, 9001), (2, 2), jnp.float32)
        _g = jnp.sign(_g) * jnp.maximum(jnp.abs(_g), 1.0) + (_g == 0) * 1.0
        g_xattn = _g[0]
        g_ffn = _g[1]
        return (x, ctx_768, g_xattn, g_ffn)
    x, ctx_768, g_xattn, g_ffn = _rec_inputs()

    def _L0_xattn_setup():
        import jax, jax.numpy as jnp
        import numpy as np
        HEADS = 8
        DIM_HEAD = 64
        QUERY_DIM = 128
        CONTEXT_DIM = 96
        INNER = HEADS * DIM_HEAD
        key = jax.random.key(seed)
        ks = jax.random.split(key, 7)
        B, Sq, Skv = (4, 512, 128)
        x = jax.random.normal(ks[0], (B, Sq, QUERY_DIM), dtype=jnp.float32)
        context = jax.random.normal(ks[1], (B, Skv, CONTEXT_DIM), dtype=jnp.float32)
        Wq = jax.random.normal(ks[2], (QUERY_DIM, INNER), dtype=jnp.float32) * QUERY_DIM ** (-0.5)
        Wk = jax.random.normal(ks[3], (CONTEXT_DIM, INNER), dtype=jnp.float32) * CONTEXT_DIM ** (-0.5)
        Wv = jax.random.normal(ks[4], (CONTEXT_DIM, INNER), dtype=jnp.float32) * CONTEXT_DIM ** (-0.5)
        Wo = jax.random.normal(ks[5], (INNER, QUERY_DIM), dtype=jnp.float32) * INNER ** (-0.5)
        bo = jax.random.normal(ks[6], (QUERY_DIM,), dtype=jnp.float32) * 0.01
        return {'x': x, 'context': context, 'Wq': Wq, 'Wk': Wk, 'Wv': Wv, 'Wo': Wo, 'bo': bo}
    _L0_xattn_all = _L0_xattn_setup()
    _L0_xattn_in = {k: v for k, v in _L0_xattn_all.items() if k in ('Wq', 'Wk', 'Wv', 'Wo', 'bo')}
    del _L0_xattn_all

    def _L0_ffn_setup():
        import jax, jax.numpy as jnp
        import numpy as np
        NUM_HEADS = 16
        TOP_K = 2
        key = jax.random.key(seed)
        ks = jax.random.split(key, 5)
        B, S, D, E = (4, 256, 128, 8)
        scale = 0.02
        return {'x': jax.random.normal(ks[0], (B, S, D), dtype=jnp.float32), 'W_qkv': jax.random.normal(ks[1], (D, 3 * D), dtype=jnp.float32) * scale, 'b_qkv': jnp.zeros((3 * D,), dtype=jnp.float32), 'W_gate': jax.random.normal(ks[2], (D, E), dtype=jnp.float32) * scale, 'b_gate': jnp.zeros((E,), dtype=jnp.float32), 'W_experts': jax.random.normal(ks[3], (E, D, D), dtype=jnp.float32) * scale, 'b_experts': jnp.zeros((E, D), dtype=jnp.float32)}
    _L0_ffn_all = _L0_ffn_setup()
    _L0_ffn_in = {k: v for k, v in _L0_ffn_all.items() if k in ('W_qkv', 'b_qkv', 'W_gate', 'b_gate', 'W_experts', 'b_experts')}
    del _L0_ffn_all

    def _L1_xattn_setup():
        import jax, jax.numpy as jnp
        import numpy as np
        N_HEAD = 16
        D_EMBED = 128
        D_CROSS = 96
        D_HEAD = D_EMBED // N_HEAD
        key = jax.random.key(seed)
        ks = jax.random.split(key, 8)
        B, SQ, SKV = (2, 512, 256)
        s_q = 1.0 / np.sqrt(D_EMBED)
        s_kv = 1.0 / np.sqrt(D_CROSS)
        return {'x': jax.random.normal(ks[0], (B, SQ, D_EMBED), jnp.float32), 'y': jax.random.normal(ks[1], (B, SKV, D_CROSS), jnp.float32), 'Wq': jax.random.normal(ks[2], (D_EMBED, D_EMBED), jnp.float32) * s_q, 'bq': jnp.zeros((D_EMBED,), jnp.float32), 'Wkv': jax.random.normal(ks[3], (D_CROSS, 2 * D_EMBED), jnp.float32) * s_kv, 'bkv': jnp.zeros((2 * D_EMBED,), jnp.float32), 'Wo': jax.random.normal(ks[4], (D_EMBED, D_EMBED), jnp.float32) * s_q, 'bo': jnp.zeros((D_EMBED,), jnp.float32)}
    _L1_xattn_all = _L1_xattn_setup()
    _L1_xattn_in = {k: v for k, v in _L1_xattn_all.items() if k in ('Wq', 'bq', 'Wkv', 'bkv', 'Wo', 'bo')}
    del _L1_xattn_all

    def _L1_ffn_setup():
        import jax, jax.numpy as jnp
        import numpy as np
        K_TOP = 2
        key = jax.random.key(seed)
        k1, k2, k3 = jax.random.split(key, 3)
        B, S, H, E = (4, 256, 128, 8)
        hidden_states = jax.random.normal(k1, (B, S, H), dtype=jnp.float32)
        router_w = jax.random.normal(k2, (E, H), dtype=jnp.float32) * 0.02
        expert_weights = jax.random.normal(k3, (E, H, H), dtype=jnp.float32) * 0.02
        return {'hidden_states': hidden_states, 'router_w': router_w, 'expert_weights': expert_weights}
    _L1_ffn_all = _L1_ffn_setup()
    _L1_ffn_in = {k: v for k, v in _L1_ffn_all.items() if k in ('router_w', 'expert_weights')}
    del _L1_ffn_all
    return {'x': x, 'ctx_768': ctx_768, 'g_xattn': g_xattn, 'g_ffn': g_ffn, 'L0_xattn_Wq': _L0_xattn_in['Wq'], 'L0_xattn_Wk': _L0_xattn_in['Wk'], 'L0_xattn_Wv': _L0_xattn_in['Wv'], 'L0_xattn_Wo': _L0_xattn_in['Wo'], 'L0_xattn_bo': _L0_xattn_in['bo'], 'L0_ffn_W_qkv': _L0_ffn_in['W_qkv'], 'L0_ffn_b_qkv': _L0_ffn_in['b_qkv'], 'L0_ffn_W_gate': _L0_ffn_in['W_gate'], 'L0_ffn_b_gate': _L0_ffn_in['b_gate'], 'L0_ffn_W_experts': _L0_ffn_in['W_experts'], 'L0_ffn_b_experts': _L0_ffn_in['b_experts'], 'L1_xattn_Wq': _L1_xattn_in['Wq'], 'L1_xattn_bq': _L1_xattn_in['bq'], 'L1_xattn_Wkv': _L1_xattn_in['Wkv'], 'L1_xattn_bkv': _L1_xattn_in['bkv'], 'L1_xattn_Wo': _L1_xattn_in['Wo'], 'L1_xattn_bo': _L1_xattn_in['bo'], 'L1_ffn_router_w': _L1_ffn_in['router_w'], 'L1_ffn_expert_weights': _L1_ffn_in['expert_weights']}

def reference(x, ctx_768, g_xattn, g_ffn, L0_xattn_Wq, L0_xattn_Wk, L0_xattn_Wv, L0_xattn_Wo, L0_xattn_bo, L0_ffn_W_qkv, L0_ffn_b_qkv, L0_ffn_W_gate, L0_ffn_b_gate, L0_ffn_W_experts, L0_ffn_b_experts, L1_xattn_Wq, L1_xattn_bq, L1_xattn_Wkv, L1_xattn_bkv, L1_xattn_Wo, L1_xattn_bo, L1_ffn_router_w, L1_ffn_expert_weights):
    import jax
    import jax.numpy as jnp

    def _L0_xattn_ref(x, context, Wq, Wk, Wv, Wo, bo):
        import jax, jax.numpy as jnp
        import numpy as np
        HEADS = 8
        DIM_HEAD = 64
        QUERY_DIM = 128
        CONTEXT_DIM = 96
        INNER = HEADS * DIM_HEAD
        B, Sq, _ = x.shape
        h, d = (HEADS, DIM_HEAD)
        scale = d ** (-0.5)
        q = (x @ Wq).reshape(B, Sq, h, d).transpose(0, 2, 1, 3)
        k = (context @ Wk).reshape(B, -1, h, d).transpose(0, 2, 1, 3)
        v = (context @ Wv).reshape(B, -1, h, d).transpose(0, 2, 1, 3)
        scores = jnp.einsum('bhid,bhjd->bhij', q, k) * scale
        attn = jax.nn.softmax(scores, axis=-1)
        out = jnp.einsum('bhij,bhjd->bhid', attn, v)
        out = out.transpose(0, 2, 1, 3).reshape(B, Sq, h * d)
        return out @ Wo + bo

    def _L0_ffn_ref(x, W_qkv, b_qkv, W_gate, b_gate, W_experts, b_experts):
        import jax, jax.numpy as jnp
        import numpy as np
        NUM_HEADS = 16
        TOP_K = 2
        B, S, D = x.shape
        H = NUM_HEADS
        hd = D // H
        E = W_gate.shape[-1]
        qkv = (x @ W_qkv + b_qkv).reshape(B, S, 3, H, hd)
        q, k, v = (qkv[:, :, 0], qkv[:, :, 1], qkv[:, :, 2])
        attn = jnp.einsum('bqhd,bkhd->bhqk', q, k) / jnp.sqrt(jnp.asarray(hd, x.dtype))
        attn = jax.nn.softmax(attn, axis=-1)
        attn_out = jnp.einsum('bhqk,bkhd->bqhd', attn, v).reshape(B, S, D)
        gate = jax.nn.softmax(x @ W_gate + b_gate, axis=-1)
        top_g, top_i = jax.lax.top_k(gate, TOP_K)
        combine = jnp.sum(jax.nn.one_hot(top_i, E, dtype=x.dtype) * top_g[..., None], axis=2)
        expert_out = jnp.einsum('bsd,edf->bsef', x, W_experts) + b_experts
        moe_out = jnp.einsum('bsef,bse->bsf', expert_out, combine)
        return attn_out + moe_out

    def _L1_xattn_ref(x, y, Wq, bq, Wkv, bkv, Wo, bo):
        import jax, jax.numpy as jnp
        import numpy as np
        N_HEAD = 16
        D_EMBED = 128
        D_CROSS = 96
        D_HEAD = D_EMBED // N_HEAD
        B, SQ, _ = x.shape
        q = x @ Wq + bq
        kv = y @ Wkv + bkv
        k, v = jnp.split(kv, 2, axis=-1)
        q = q.reshape(B, SQ, N_HEAD, D_HEAD).transpose(0, 2, 1, 3)
        k = k.reshape(B, -1, N_HEAD, D_HEAD).transpose(0, 2, 1, 3)
        v = v.reshape(B, -1, N_HEAD, D_HEAD).transpose(0, 2, 1, 3)
        scale = 1.0 / np.sqrt(D_HEAD)
        attn = jnp.einsum('bhqd,bhkd->bhqk', q, k) * scale
        attn = jax.nn.softmax(attn, axis=-1)
        out = jnp.einsum('bhqk,bhkd->bhqd', attn, v)
        out = out.transpose(0, 2, 1, 3).reshape(B, SQ, D_EMBED)
        return out @ Wo + bo

    def _L1_ffn_ref(hidden_states, router_w, expert_weights):
        import jax, jax.numpy as jnp
        import numpy as np
        K_TOP = 2
        B, S, H = hidden_states.shape
        x = hidden_states.reshape(-1, H)
        logits = x @ router_w.T
        probs = jax.nn.softmax(logits, axis=-1)
        topk_vals, topk_idx = jax.lax.top_k(probs, K_TOP)
        topk_w = topk_vals / (topk_vals.sum(-1, keepdims=True) + 1e-06)
        expert_out = jnp.einsum('nh,eho->eno', x, expert_weights)
        combined = jnp.take_along_axis(expert_out.transpose(1, 0, 2), topk_idx[:, :, None], axis=1)
        combined = combined.transpose(1, 0, 2)
        remap_bias = jnp.take_along_axis(probs, topk_idx, axis=1).T[:, :, None]
        weights = topk_w.T[:, :, None]
        out = ((combined + remap_bias) * weights).sum(axis=0)
        return out.reshape(B, S, H)
    x = x + jnp.tanh(g_xattn[0]) * _L0_xattn_ref(_layernorm(x, axis=-1), ctx_768, L0_xattn_Wq, L0_xattn_Wk, L0_xattn_Wv, L0_xattn_Wo, L0_xattn_bo)
    x = x + jnp.tanh(g_ffn[0]) * _L0_ffn_ref(_layernorm(x, axis=-1), L0_ffn_W_qkv, L0_ffn_b_qkv, L0_ffn_W_gate, L0_ffn_b_gate, L0_ffn_W_experts, L0_ffn_b_experts)
    x = x + jnp.tanh(g_xattn[1]) * _L1_xattn_ref(_layernorm(x, axis=-1), ctx_768, L1_xattn_Wq, L1_xattn_bq, L1_xattn_Wkv, L1_xattn_bkv, L1_xattn_Wo, L1_xattn_bo)
    x = x + jnp.tanh(g_ffn[1]) * _L1_ffn_ref(_layernorm(x, axis=-1), L1_ffn_router_w, L1_ffn_expert_weights)
    return x

_drawn_inputs = setup_inputs


def setup_inputs(seed=0):
    import zlib

    import numpy as np

    out = dict(_drawn_inputs(seed))
    spreads = {'g_ffn': (-1.0, 0.6),
     'L0_ffn_b_qkv': (0.0, 0.1),
     'L0_ffn_b_gate': (0.0, 0.391),
     'L0_ffn_b_experts': (0.0, 0.416),
     'L1_xattn_bq': (0.0, 0.334),
     'L1_xattn_bkv': (0.0, 0.1),
     'L1_xattn_bo': (0.0, 0.1)}
    factors = {'L0_xattn_bo': 4.949}
    for name, (base, spread) in spreads.items():
        noise = np.random.default_rng([zlib.crc32(name.encode()), seed]).standard_normal(out[name].shape)
        drawn = base * np.exp(spread * noise) if base else spread * noise
        out[name] = jnp.asarray(drawn.astype(out[name].dtype))
    for name, factor in factors.items():
        out[name] = (out[name] * factor).astype(out[name].dtype)
    return out
```

```python
from contextlib import ExitStack

import numpy as np
import concourse.bass as bass
from concourse import mybir

ALU = mybir.AluOpType
ACT = mybir.ActivationFunctionType
AX = mybir.AxisListType
F32 = mybir.dt.float32
BF16 = mybir.dt.bfloat16
U32 = mybir.dt.uint32

P = 128
BATCH, SEQ, KV, CD = 8, 256, 512, 96
QT = SEQ // P
XH, XD = 8, 64
H8, D8 = 16, 8
NPAIR = H8 // 2
NE = 8
KROWS = 6 * D8
MROWS = KROWS + 2
SLOTS = 8
EPS = 1e-5
QPART = (0, 1, 2, 0, 1, 0)
KPART = (0, 0, 0, 1, 1, 2)

KEYS = {"A": SEQ, "B": KV}


def stream_steps(s):
    st = []
    if s == "A":
        st += [("ln", 0, .3, "sm", .4, 2.5), ("qp", 0, 1.7, "st", 1.1, .7), ("qp", 1, 1.7, "st", 1.1, 0)]
        st += [("mx", k, .22, "sm", .62, .9 if k == 0 else 0) for k in range(XH * QT)]
        st += [("mT", 0, .2, "sm", .4, .8), ("vp", 0, 1.7, "st", 1.1, 0), ("vp", 1, 1.7, "st", 1.1, 0)]
        for u in range(XH):
            st.append(("e", u, 1.75, "st", 1.1, 1.5 if u == 0 else 0))
            if u % 2 == 1 and u > 1:
                st.append(("pv", u // 2 - 1, 2.3, "", 0, 0))
        st += [("pv", XH // 2 - 1, 2.3, "", 0, 2.5), ("out", 0, 1.8, "sm", .5, 1.2)]
        st += [("ln", 1, .3, "sm", .4, 2.5), ("qk", 0, .9, "st", 1.2, .6), ("v8", 0, .5, "sm", .5, 0),
               ("gate", 0, .1, "sm", 3., 0)]
        st += [("moe", k, .9, "sm", .8, .2) for k in range(4)]
        st += [("mx8", k, .22, "sm", .62, 4. if k == 0 else 0) for k in range(H8)]
        st += [("mT8", 0, .2, "sm", .6, .8), ("wT", 0, .2, "sm", .4, 0)]
        for u in range(NPAIR):
            st.append(("e8", u, .45, "st", 1.1, 4.5 if u == 0 else 0))
            if u % 2 == 1 and u > 1:
                st.append(("pv8", u // 2 - 1, 1.1, "", 0, 0))
        st += [("pv8", 3, 1.1, "", 0, 1.2), ("out8", 0, 1.8, "sm", .5, 2.5)]
    else:
        st += [("ln", 0, .3, "sm", .4, 2.5), ("qk", 0, 1.3, "st", 1.4, .6), ("v8", 0, .5, "sm", .5, 0),
               ("v8", 1, .5, "sm", .5, 0)]
        st += [("mx8", k, .22, "sm", .62, 9. if k == 0 else 0) for k in range(H8 * QT)]
        st += [("mT8", 0, .2, "sm", .6, .8)]
        for u in range(2 * NPAIR):
            st.append(("e8", u, .45, "st", 1.1, 5. if u == 0 else 0))
            if u % 4 == 3 and u > 4:
                st.append(("pv8", u // 4 - 1, 2.2, "", 0, 0))
            elif u == 1 and False:
                pass
        st += [("pv8", 3, 2.2, "", 0, 1.2), ("out8", 0, 1.8, "sm", .5, 2.5)]
        st += [("ln", 1, .3, "sm", .4, 2.5), ("gate", 0, .1, "sm", 3., .6)]
        st += [("moe", k, .9, "sm", .8, .2) for k in range(4)]
    return st


def merge(streams):
    at = {s: 0 for s in streams}
    steps = {s: stream_steps(s) for s in streams}
    ready = {s: 0. for s in streams}
    pe = 0.
    ring = {"st": [0., 0.], "sm": [0., 0.]}
    order = []
    while any(at[s] < len(steps[s]) for s in streams):
        best = None
        for s in streams:
            if at[s] < len(steps[s]):
                name, k, cost, cons, took, gap = steps[s][at[s]]
                start = max(pe, ready[s] + gap, ring[cons][-2] if cons else 0.)
                left = len(steps[s]) - at[s]
                if best is None or (start, -left) < best[0]:
                    best = ((start, -left), s)
        s = best[1]
        start = best[0][0]
        name, k, cost, cons, took, gap = steps[s][at[s]]
        at[s] += 1
        pe = start + cost
        if cons:
            ring[cons].append(max(ring[cons][-1], pe) + took)
            nxt = steps[s][at[s]] if at[s] < len(steps[s]) else None
            ready[s] = pe if nxt is None or nxt[5] == 0 else ring[cons][-1]
        else:
            ready[s] = pe
        order.append((s, name, k, cons))
    return order


ORDER = {"A": merge("A"), "B": merge("B"), "AB": merge("AB")}
RINGS = {s: {r: sum(o[3] == r for o in merge(s)) for r in ("st", "sm")} for s in "AB"}

COUNTS = dict(
    xin=16, ctx=16, xb=1, mv=2, rstd=2, xh=2, qab=2, ctb=1, mroww=16, mrowr=16, psum=XH, pv=XH // 2, norm=XH // 2,
    split=1, splitw=16, qks=18 * 16, lg=1, eg=1, w=1, xb2=1, m2w=16, m2r=32, pv8=4, norm8=2, out=16,
    pch={"A": 17, "B": 9}, vch={"A": 19, "B": 21})


CREDIT = {("B", "xb2"): 1, ("B", "out"): 16}


def build(nc, a, out):
    ctx = ExitStack()
    with ctx:
        def sb(name, shape, dt=F32):
            return ctx.enter_context(nc.sbuf_tensor(name, shape, dt))

        def dram(name, shape, dt):
            return nc.dram_tensor(name, shape, dt, kind="Internal").ap()

        def sem(name):
            return ctx.enter_context(nc.semaphore(name))

        ident = sb("ident", [P, P])
        sel = sb("sel", [P, 4 * D8])
        iota = sb("iota", [P, NE])
        ones = sb("ones", [P, XD])
        wqk = sb("wqk", [P, XH, CD])
        wvx = sb("wvx", [CD, XH * XD])
        wox = sb("wox", [P, XH // 2, P])
        gates = sb("gates", [P, 4])
        graw = sb("graw", [P, 4])
        bo = {s: sb("bo" + s, [P, P]) for s in "AB"}
        wq8 = {s: sb("wq8" + s, [P, P]) for s in "AB"}
        wk8 = {"A": sb("wk8A", [P, P]), "B": sb("wk8B", [CD, P])}
        wv8 = {"A": sb("wv8A", [P, P]), "B": sb("wv8B", [CD, P])}
        bq8 = {s: sb("bq8" + s, [P, 2]) for s in "AB"}
        bv8 = {s: sb("bv8" + s, [P, P]) for s in "AB"}
        wo8 = sb("wo8", [P, 4, P])
        wg = {s: sb("wg" + s, [P, NE]) for s in "AB"}
        bg = sb("bg", [P, NE])
        we = {s: sb("we" + s, [P, NE * P]) for s in "AB"}
        be = sb("be", [NE, P])
        nhalf = sb("nhalf", [P, QT])

        def per(name, shape, dt=F32):
            return {s: sb(name + s, shape, dt) for s in "AB"}

        xin = {"A": sb("xinA", [P, QT, P]), "B": sb("xmid", [P, QT, P])}
        cT = {s: sb("cT" + s, [CD + 1, KV]) for s in "AB"}
        xb = per("xb", [P, QT, P])
        x1 = per("x1", [P, QT, P])
        st6 = per("st6", [P, QT, 6])
        mv = per("mv", [P, QT, 2])
        ve = per("ve", [P, QT])
        rstd = per("rstd", [P, QT])
        xh = per("xh", [P, QT, P])
        xT = per("xT", [P, SEQ])
        qA = sb("qA", [CD + 1, XH, SEQ])
        qAb = sb("qAb", [CD, XH, SEQ], BF16)
        cTb = sb("cTb", [CD, KV], BF16)
        vX = sb("vX", [P, KV // P, XH * XD])
        mxA = sb("mxA", [P, QT, XH])
        mrow = sb("mrow", [XH, SEQ])
        prob = {s: [sb(f"prob{s}{n}", [P, 4 * SEQ]) for n in range(SLOTS)] for s in "AB"}
        wqT = prob["A"][0][0:XD, 0:XH * P].rearrange("p (h n) -> p h n", h=XH)
        wkT = prob["A"][1][0:XD, 0:XH * CD].rearrange("p (h n) -> p h n", h=XH)
        half = sb("half", [P, 2 * SEQ])
        psum_k = [sb(f"psum_k{n}", [P, SEQ]) for n in range(4)]
        rden = per("rden", [P, 2 * SEQ])
        oTX = sb("oTX", [P, XH // 2, SEQ])
        qk = {s: sb("qk" + s, [P, SEQ + KEYS[s]]) for s in "AB"}
        parts = {s: sb("parts" + s, [P, 3, SEQ + KEYS[s]], BF16) for s in "AB"}
        q8 = {s: sb("q8" + s, [P, NPAIR, SEQ], BF16) for s in "AB"}
        k8 = {s: sb("k8" + s, [P, NPAIR, KEYS[s]], BF16) for s in "AB"}
        v8 = {s: sb("v8" + s, [P, KEYS[s] // P, H8, 32]) for s in "AB"}
        mx8 = per("mx8", [P, QT, H8])
        m2 = per("m2", [H8, 2, SEQ], BF16)
        oT8 = per("oT8", [P, 4, SEQ])
        lg = per("lg", [P, QT, NE])
        nm = per("nm", [P, QT])
        eg = per("eg", [P, QT, NE])
        sg = per("sg", [P, QT])
        pr = per("pr", [P, QT, NE])
        top = per("top", [P, QT, 8])
        tix = per("tix", [P, QT, 8], U32)
        tif = per("tif", [P, QT, 8])
        w0 = per("w0", [P, QT, NE])
        w1 = per("w1", [P, QT, NE])
        w = per("w", [P, QT, NE])
        ts = sb("ts", [P, QT])
        wp = sb("wp", [P, QT, NE])
        cb = sb("cb", [P, QT])
        wT = sb("wT", [NE, SEQ])
        prod = {"A": [vX[:, 2 * t:2 * t + 2, :].rearrange("p c n -> p (c n)") for t in range(QT)],
                "B": [oT8["B"][:].rearrange("p g n -> p (g n)"), sb("prodB1", [P, NE * P])[:]]}
        fin = per("fin", [P, QT, P])

        mrow_d = dram("mrow_d", [XH, SEQ], F32)
        part_d = {s: dram("part_d" + s, [3, P, SEQ + KEYS[s]], BF16) for s in "AB"}
        m2_d = {s: dram("m2_d" + s, [2, H8, SEQ], BF16) for s in "AB"}

        st = ctx.enter_context(nc.psum_tensor("st", [P, 2, 1024], F32))
        sm = ctx.enter_context(nc.psum_tensor("sm", [P, 2, 512], F32))
        pvb = {s: ctx.enter_context(nc.psum_tensor("pv" + s, [P, 512], F32)) for s in "AB"}

        ring_full = {r: sem(r + "_full") for r in ("st", "sm")}
        ring_done = {r: sem(r + "_done") for r in ("st", "sm")}
        ring_psum = {"st": st, "sm": sm}
        S = {s: {n: sem(n + s) for n in COUNTS} for s in "AB"}
        w_loaded, c_set, tanh_done, bias_done = sem("w_loaded"), sem("c_set"), sem("tanh_done"), sem("bias_done")
        passed = sem("passed")
        fold_ps, fold_ev = sem("fold_ps"), sem("fold_ev")

        cnt = {}
        for s in "AB":
            cnt[s] = {n: c[s] if isinstance(c, dict) else c for n, c in COUNTS.items()}

        class Stream:

            def __init__(self, s, batch, base, places):
                self.s, self.batch, self.base, self.places = s, batch, base, places

            def value(self, n, k):
                return self.batch * cnt[self.s][n] + (k + CREDIT.get((self.s, n), 0))

            def place(self, name, k):
                ring, n = self.places[self.s, name, k]
                reg, const = self.base[ring]
                return ring, reg, const + n

            def slot(self, name, k):
                ring, _, n = self.place(name, k)
                return ring_psum[ring][:, n % 2, :]

            def full(self, name, k):
                ring, reg, n = self.place(name, k)
                return ring_full[ring], reg + (n + 1)

            def done(self, name, k=0):
                ring, reg, n = self.place(name, k)
                return ring_done[ring], reg + (n + 1)

            def before(self, ring):
                reg, const = self.base[ring]
                return ring_done[ring], reg + const

        def run(eng, step):
            def steps(streams, batch_a, batch_b, base):
                places, n = {}, {r: 0 for r in base}
                for s, name, k, cons in ORDER[streams]:
                    if cons:
                        places[s, name, k] = (cons, n[cons])
                        n[cons] += 1
                batch = {"A": Stream("A", batch_a, base, places), "B": Stream("B", batch_b, base, places)}
                for s, name, k, cons in ORDER[streams]:
                    step(batch[s], name, k, cons)

            tot = {r: RINGS["A"][r] + RINGS["B"][r] for r in ("st", "sm")}
            assert all(t % 2 == 0 for t in tot.values())
            steps("A", 0, 0, {r: (0, 0) for r in tot})
            with eng.Fori(0, BATCH - 1) as i:
                steps("AB", i + 1, i, {r: (i * tot[r], RINGS["A"][r]) for r in tot})
            steps("B", BATCH - 1, BATCH - 1, {r: (0, RINGS["A"][r] + (BATCH - 1) * tot[r]) for r in tot})

        NC = {s: KEYS[s] // P for s in "AB"}
        block = ctx.enter_context(nc.Block())

        def apart(eng):
            eng.sem_inc(passed, 1)

        W_LOADS = 0
        loads = [(ident[:], a["ident"]), (wqT, a["wqT"]), (wkT, a["wkT"]),
                 (graw[:, 0:2], a["g_xattn"].rearrange("(o n) -> o n", o=1).broadcast_to([P, 2])),
                 (graw[:, 2:4], a["g_ffn"].rearrange("(o n) -> o n", o=1).broadcast_to([P, 2])),
                 (sel[:], a["sel"]), (iota[:], a["iota"]), (wvx[:], a["wvx"]), (wox[:], a["wox"]),
                 (be[:], a["be"]), (bg[:], a["bg"].rearrange("(o n) -> o n", o=1).broadcast_to([P, NE]))]
        for s in "AB":
            loads += [(bo[s][:], a["bo" + s].rearrange("(o n) -> o n", o=1).broadcast_to([P, P])),
                      (wq8[s][:], a["wq8" + s]), (wk8[s][:], a["wk8" + s]), (wv8[s][:], a["wv8" + s]),
                      (bq8[s][:], a["bq8" + s]),
                      (bv8[s][:], a["bv8" + s].rearrange("(o n) -> o n", o=1).broadcast_to([P, P])),
                      (wg[s][:], a["wg" + s]), (we[s][:].rearrange("p (e n) -> p e n", e=NE), a["we" + s].rearrange("e k n -> k e n"))]
        W_LOADS = 16 * (len(loads) + 4)
        MEMSETS = 7

        @block.sync
        def _(sp):
            for dst, src in loads:
                sp.dma_start(dst, src).then_inc(w_loaded, 16)
            sp.wait_ge(c_set, MEMSETS)
            for i in range(4):
                sp.dma_start(wo8[32 * i:32 * i + D8], a["wo8"].rearrange("(g i d) n -> i d g n", g=4, i=4)[i])\
                    .then_inc(w_loaded, 16)

            def step(b, name, k, cons):
                s, sm_ = b.s, S[b.s]
                if name == "ln" and k == 0:
                    if s == "A":
                        sp.wait_ge(*b.before("sm"))
                        sp.dma_start(xin["A"][:], a["x"][bass.ds(b.batch, 1)].rearrange("o (t p) n -> p (o t) n", p=P))\
                            .then_inc(sm_["xin"], 16)
                    else:
                        sp.wait_ge(*b.before("sm"))
                    sp.wait_ge(*b.before("st"))
                    sp.dma_start(cT[s][0:CD], a["ctxT"][bass.ds(b.batch, 1)].rearrange("o c t -> (o c) t"))\
                        .then_inc(sm_["ctx"], 16)
                if name == "mT":
                    sp.wait_ge(*b.done("mT"))
                    sp.dma_start(mrow_d, mrow[:]).then_inc(sm_["mroww"], 16)
                    sp.wait_ge(sm_["mroww"], b.value("mroww", 16))
                    sp.dma_start(qA[CD:CD + 1], mrow_d.rearrange("(o h) n -> o h n", o=1)).then_inc(sm_["mrowr"], 16)
                if name == "qk":
                    sp.wait_ge(sm_["split"], b.value("split", 1))
                    sp.dma_start(part_d[s].rearrange("t p n -> p t n"), parts[s][:]).then_inc(sm_["splitw"], 16)
                    sp.wait_ge(sm_["splitw"], b.value("splitw", 16))
                    src = part_d[s].rearrange("t (d p i) n -> i (t d) p n", i=2, p=NPAIR)
                    for i in range(2):
                        for j0, n in ((0, 3), (3, 2), (5, 1)):
                            r = 64 * i + D8 * j0
                            sp.dma_start(q8[s][r:r + D8 * n], src[i, 0:D8 * n, :, 0:SEQ]).then_inc(sm_["qks"], 16)
                        for j in range(6):
                            r, t = 64 * i + D8 * j, D8 * KPART[j]
                            sp.dma_start(k8[s][r:r + D8], src[i, t:t + D8, :, SEQ:]).then_inc(sm_["qks"], 16)
                if name == "mT8":
                    sp.wait_ge(*b.done("mT8"))
                    sp.dma_start(m2_d[s].rearrange("t h n -> h t n"), m2[s][:]).then_inc(sm_["m2w"], 16)
                    sp.wait_ge(sm_["m2w"], b.value("m2w", 16))
                    for i in range(2):
                        sp.dma_start(q8[s][64 * i + KROWS:64 * i + MROWS],
                                     m2_d[s].rearrange("t (p i) n -> i t p n", i=2)[i]).then_inc(sm_["m2r"], 16)
                if name == "moe" and k == 3 and s == "B":
                    sp.wait_ge(sm_["xb2"], b.value("xb2", 1))
                    sp.dma_start(out[bass.ds(b.batch, 1)].rearrange("o (t p) n -> p (o t) n", p=P), fin["B"][:])\
                        .then_inc(sm_["out"], 16)
            run(sp, step)
            sp.wait_ge(S["B"]["out"], 16 * BATCH + CREDIT["B", "out"])

        @block.tensor
        def _(pe):
            pe.wait_ge(w_loaded, W_LOADS)
            pe.wait_ge(c_set, MEMSETS)
            for h in range(XH):
                fold = nc.tensor.matmul(st[:, h // 4, (h % 4) * P:(h % 4) * P + CD], wqT[:, h, :], wkT[:, h, :],
                                        start=True, stop=True)
            fold.then_inc(fold_ps, 1)
            pe.wait_ge(fold_ev, 2)

            def step(b, name, k, cons):
                s, m = b.s, S[b.s]
                if cons:
                    ring, reg, n = b.place(name, k)
                    if not isinstance(reg, int) or n >= 2:
                        pe.wait_ge(ring_done[ring], reg + (n - 1))
                    ps = b.slot(name, k)
                if name == "ln":
                    pe.wait_ge(m["xh"], b.value("xh", k + 1))
                    for t in range(QT):
                        last = nc.tensor.transpose(ps[:, t * P:(t + 1) * P], xh[s][:, t, :], ident[:])
                elif name == "qp":
                    pe.wait_ge(*b.done("ln", 0))
                    for j in range(4):
                        last = nc.tensor.matmul(ps[0:CD, j * SEQ:(j + 1) * SEQ], wqk[:, 4 * k + j, :], xT[s][:],
                                                start=True, stop=True)
                elif name == "vp":
                    pe.wait_ge(m["ctx"], b.value("ctx", 16))
                    for j in range(2):
                        c = 2 * k + j
                        last = nc.tensor.matmul(ps[:, j * 512:(j + 1) * 512], cT[s][0:CD, c * P:(c + 1) * P], wvx[:],
                                                start=True, stop=True)
                elif name == "mx":
                    h, t = divmod(k, QT)
                    pe.wait_ge(m["qab"], b.value("qab", h // 4 + 1))
                    pe.wait_ge(m["ctb"], b.value("ctb", 1))
                    last = nc.tensor.matmul(ps, qAb[:, h, t * P:(t + 1) * P], cTb[:], start=True, stop=True)
                elif name == "mT":
                    pe.wait_ge(*b.done("mx", XH * QT - 1))
                    for t in range(QT):
                        last = nc.tensor.transpose(ps[0:XH, t * P:(t + 1) * P], mxA[:, t, :], ident[:])
                elif name == "e":
                    pe.wait_ge(m["mrowr"], b.value("mrowr", 16))
                    for c in range(KV // P):
                        last = nc.tensor.matmul(ps[:, c * SEQ:(c + 1) * SEQ], cT[s][:, c * P:(c + 1) * P], qA[:, k, :],
                                                start=True, stop=True)
                elif name == "pv":
                    pe.wait_ge(*b.done("e", 2 * k + 1))
                    pe.wait_ge(*b.done("vp", 1))
                    if k > 0:
                        pe.wait_ge(m["norm"], b.value("norm", k))
                    pv = pvb[s]
                    for c in range(KV // P):
                        for i in range(2):
                            h = 2 * k + i
                            nc.tensor.matmul(pv[64 * i:64 * i + 64, 0:SEQ], vX[:, c, h * XD:(h + 1) * XD],
                                             prob[s][h][:, c * SEQ:(c + 1) * SEQ], start=(c == 0), stop=(c == KV // P - 1))
                    pe.wait_ge(m["psum"], b.value("psum", 2 * k + 2))
                    for i in range(2):
                        last = nc.tensor.matmul(pv[64 * i:64 * i + 64, SEQ:2 * SEQ], ones[:], psum_k[(2 * k + i) % 4][:],
                                                start=True, stop=True)
                    last.then_inc(m["pv"], 1)
                elif name == "out":
                    pe.wait_ge(m["norm"], b.value("norm", XH // 2))
                    for t in range(QT):
                        for j in range(XH // 2):
                            last = nc.tensor.matmul(ps[:, t * P:(t + 1) * P], oTX[:, j, t * P:(t + 1) * P], wox[:, j, :],
                                                    start=(j == 0), stop=(j == XH // 2 - 1))
                elif name == "qk":
                    pe.wait_ge(m["ctx"], b.value("ctx", 16))
                    pe.wait_ge(*b.done("ln", 1 if s == "A" else 0))
                    keys_from = xT[s][:] if s == "A" else cT[s][0:CD, :]
                    nc.tensor.matmul(ps[:, 0:SEQ], wq8[s][:], xT[s][:], start=True, stop=True)
                    last = nc.tensor.matmul(ps[:, 512:512 + KEYS[s]], wk8[s][:], keys_from, start=True, stop=True)
                elif name == "v8":
                    pe.wait_ge(*b.done("ln", 1 if s == "A" else 0))
                    pe.wait_ge(m["ctx"], b.value("ctx", 16))
                    for j in range(2):
                        c = 2 * k + j
                        tok = xT[s][:, c * P:(c + 1) * P] if s == "A" else cT[s][0:CD, c * P:(c + 1) * P]
                        last = nc.tensor.matmul(ps[:, j * P:(j + 1) * P], tok, wv8[s][:], start=True, stop=True)
                elif name == "gate":
                    pe.wait_ge(*b.done("ln", 1))
                    for t in range(QT):
                        last = nc.tensor.matmul(ps[:, t * NE:(t + 1) * NE], xT[s][:, t * P:(t + 1) * P], wg[s][:],
                                                start=True, stop=True)
                elif name == "moe":
                    t, f = divmod(k, 2)
                    last = nc.tensor.matmul(ps, xT[s][:, t * P:(t + 1) * P], we[s][:, f * 512:(f + 1) * 512],
                                            start=True, stop=True)
                elif name == "mx8":
                    pe.wait_ge(m["qks"], b.value("qks", 18 * 16))
                    if s == "A":
                        p, i = divmod(k, 2)
                        for t in range(QT):
                            last = nc.tensor.matmul(ps[:, t * SEQ:(t + 1) * SEQ],
                                                    q8[s][64 * i:64 * i + KROWS, p, t * P:(t + 1) * P],
                                                    k8[s][64 * i:64 * i + KROWS, p, :], start=True, stop=True)
                    else:
                        p, t, i = k // 4, k // 2 % 2, k % 2
                        last = nc.tensor.matmul(ps, q8[s][64 * i:64 * i + KROWS, p, t * P:(t + 1) * P],
                                                k8[s][64 * i:64 * i + KROWS, p, :], start=True, stop=True)
                elif name == "mT8":
                    pe.wait_ge(*b.done("mx8", H8 * NC[s] // 2 - 1))
                    for t in range(QT):
                        last = nc.tensor.transpose(ps[0:H8, t * P:(t + 1) * P], mx8[s][:, t, :], ident[:])
                elif name == "wT":
                    pe.wait_ge(m["w"], b.value("w", 1))
                    for t in range(QT):
                        last = nc.tensor.transpose(ps[0:NE, t * P:(t + 1) * P], w[s][:, t, :], ident[:])
                elif name == "e8":
                    pe.wait_ge(m["m2r"], b.value("m2r", 32))
                    p, c0 = (k, 0) if s == "A" else (k // 2, 2 * (k % 2))
                    for c in range(2):
                        for i in range(2):
                            last = nc.tensor.matmul(ps[:, 512 * i + SEQ * c:512 * i + SEQ * (c + 1)],
                                                    k8[s][64 * i:64 * i + MROWS, p, (c0 + c) * P:(c0 + c + 1) * P],
                                                    q8[s][64 * i:64 * i + MROWS, p, :], start=True, stop=True)
                elif name == "pv8":
                    n = NC[s]
                    pe.wait_ge(*b.done("e8", n * (k + 1) - 1))
                    pe.wait_ge(*b.done("v8", n // 2 - 1))
                    if k >= 2:
                        pe.wait_ge(m["norm8"], b.value("norm8", k // 2))
                    for c in range(n):
                        for i in range(4):
                            h = 4 * k + i
                            u = (h // 2) * (n // 2) + c // 2
                            o = 512 * (h % 2) + SEQ * (c % 2)
                            last = nc.tensor.matmul(pvb[s][32 * i:32 * i + 32, (k % 2) * SEQ:(k % 2 + 1) * SEQ],
                                                    v8[s][:, c, h, :], prob[s][u % SLOTS][:, o:o + SEQ],
                                                    start=(c == 0), stop=(c == n - 1), tile_position=(0, 32 * i))
                    last.then_inc(m["pv8"], 1)
                elif name == "out8":
                    pe.wait_ge(m["norm8"], b.value("norm8", 2))
                    if s == "A":
                        pe.wait_ge(*b.done("wT"))
                    for t in range(QT):
                        if s == "A":
                            nc.tensor.matmul(ps[:, t * P:(t + 1) * P], wT[:, t * P:(t + 1) * P], be[:],
                                             start=True, stop=False, skip_group_check=True)
                        for g in range(4):
                            if s == "A":
                                last = nc.tensor.matmul(ps[:, t * P + 32 * g:t * P + 32 * g + 32],
                                                        oT8[s][:, g, t * P:(t + 1) * P], sel[:],
                                                        start=False, stop=(g == 3), skip_group_check=True)
                            else:
                                last = nc.tensor.matmul(ps[:, t * P:(t + 1) * P], oT8[s][:, g, t * P:(t + 1) * P],
                                                        wo8[:, g, :], start=(g == 0), stop=(g == 3))
                if cons:
                    last.then_inc(ring_full[cons], 1)
            run(pe, step)

        @block.scalar
        def _(act):
            act.wait_ge(w_loaded, W_LOADS)
            nc.scalar.activation(gates[:], graw[:], ACT.Tanh).then_inc(tanh_done, 1)
            act.wait_ge(fold_ps, 1)
            for j in range(2):
                nc.scalar.activation(wqk[:, 4 * j:4 * j + 4, :],
                                     st[:, j, 0:4 * P].rearrange("p (h n) -> p h n", h=4)[:, :, 0:CD],
                                     ACT.Copy).then_inc(fold_ev, 1)

            def step(b, name, k, cons):
                s, m = b.s, S[b.s]
                if name == "gate":
                    act.wait_ge(m["lg"], b.value("lg", 1))
                    nc.scalar.activation(eg[s][:], lg[s][:], ACT.Exp).then_inc(m["eg"], 1)
                if cons != "st":
                    return
                act.wait_ge(*b.full(name, k))
                ps = b.slot(name, k)
                done = ring_done["st"]
                if name == "qp":
                    nc.scalar.activation(qA[0:CD, 4 * k:4 * k + 4, :], ps[0:CD].rearrange("p (h n) -> p h n", h=4),
                                         ACT.Copy).then_inc(done, 1)
                elif name == "vp":
                    nc.scalar.activation(vX[:, 2 * k:2 * k + 2, :], ps.rearrange("p (h n) -> p h n", h=2),
                                         ACT.Copy).then_inc(done, 1)
                elif name == "e":
                    nc.scalar.activation(prob[s][k][:], ps, ACT.Exp, scale=float(XD) ** -0.5).then_inc(done, 1)
                elif name == "qk":
                    nc.scalar.activation(qk[s][:, 0:SEQ], ps[:, 0:SEQ], ACT.Identity, bias=bq8[s][:, 0:1])
                    nc.scalar.activation(qk[s][:, SEQ:], ps[:, 512:512 + KEYS[s]], ACT.Identity,
                                         bias=bq8[s][:, 1:2]).then_inc(done, 1)
                elif name == "e8":
                    if k >= SLOTS:
                        act.wait_ge(m["pv8"], b.value("pv8", (k - SLOTS) // NC[s] + 1))
                    nc.scalar.activation(prob[s][k % SLOTS][:], ps, ACT.Exp, scale=float(D8) ** -0.5)\
                        .then_inc(done, 1)
            run(act, step)
        @block.vector
        def _(dve):
            dve.wait_ge(w_loaded, W_LOADS)

            def step(b, name, k, cons):
                s, m = b.s, S[b.s]
                if name not in ("pv", "pv8") and cons != "sm":
                    return
                calls = link_of[s]

                def link(ins):
                    calls[0] += 1
                    ins.then_inc(m["vch"], 1)
                    dve.wait_ge(m["vch"], b.value("vch", calls[0]))

                if name == "ln":
                    if k == 0:
                        calls[0] = 0
                    src = xin[s] if k == 0 else x1[s]
                    if k == 0:
                        if s == "A":
                            dve.wait_ge(m["xin"], b.value("xin", 16))
                        else:
                            dve.wait_ge(*b.before("sm"))
                    else:
                        dve.wait_ge(*b.done("out" if s == "A" else "out8"))
                    for t in range(QT):
                        last = nc.vector.bn_stats(st6[s][:, t, :], src[:, t, :])
                    link(last)
                    apart(dve)
                    for t in range(QT):
                        last = nc.vector.bn_aggr(mv[s][:, t, :], st6[s][:, t, :])
                    last.then_inc(m["mv"], 1)
                    dve.wait_ge(m["rstd"], b.value("rstd", k + 1))
                    for t in range(QT):
                        last = nc.vector.tensor_scalar(xh[s][:, t, :], src[:, t, :], mv[s][:, t, 0:1], rstd[s][:, t:t + 1],
                                                       ALU.subtract, ALU.mult)
                    last.then_inc(m["xh"], 1)
                if name == "pv":
                    dve.wait_ge(m["pv"], b.value("pv", k + 1))
                    link(nc.vector.reciprocal(rden[s][:, 0:SEQ], pvb[s][:, SEQ:2 * SEQ]))
                    nc.vector.tensor_tensor(oTX[:, k, :], pvb[s][:, 0:SEQ], rden[s][:, 0:SEQ], ALU.mult)\
                        .then_inc(m["norm"], 1)
                    return
                if name == "pv8":
                    if k % 2 == 0:
                        return
                    dve.wait_ge(m["pv8"], b.value("pv8", k + 1))
                    link(nc.vector.reciprocal(rden[s][:], pvb[s][:]))
                    apart(dve)
                    link(nc.vector.stream_shuffle(rden[s][:], rden[s][:], [D8] * 32))
                    nc.vector.tensor_tensor(oT8[s][:, k - 1:k + 1, :], pvb[s][:].rearrange("p (g n) -> p g n", g=2),
                                            rden[s][:].rearrange("p (g n) -> p g n", g=2), ALU.mult)\
                        .then_inc(m["norm8"], 1)
                    return
                dve.wait_ge(*b.full(name, k))
                ps = b.slot(name, k)
                done = ring_done["sm"]
                if name == "ln":
                    nc.vector.tensor_copy(xT[s][:], ps[:, 0:SEQ]).then_inc(done, 1)
                elif name == "mx":
                    h, t = divmod(k, QT)
                    nc.vector.tensor_reduce(mxA[:, t, h:h + 1], ps, AX.X, ALU.max, negate=True).then_inc(done, 1)
                elif name == "mT":
                    nc.vector.tensor_copy(mrow[:], ps[0:XH, 0:SEQ]).then_inc(done, 1)
                elif name == "out" or name == "out8":
                    gate = {"out": 0, "out8": 2 if s == "A" else 1}[name]
                    if name == "out" or s == "B":
                        res, dst = xb[s], x1[s]
                        dve.wait_ge(m["xb"], b.value("xb", 1))
                    else:
                        res, dst = fin[s], xin["B"]
                        dve.wait_ge(m["xb2"], b.value("xb2", 1))
                        dve.wait_ge(S["B"]["xb"], b.batch)
                    nc.vector.scalar_tensor_tensor(out=dst[:], in0=ps[:, 0:QT * P].rearrange("p (t n) -> p t n", t=QT),
                                                   scalar=gates[:, gate:gate + 1], in1=res[:],
                                                   op0=ALU.mult, op1=ALU.add).then_inc(done, 1)
                elif name == "v8":
                    ins = nc.vector.tensor_tensor(
                        v8[s][:, 2 * k:2 * k + 2, :, 0:D8],
                        ps[:, 0:2 * P].rearrange("p (c h d) -> p c h d", c=2, h=H8),
                        bv8[s][:].rearrange("p (o h d) -> p o h d", o=1, h=H8).broadcast_to([P, 2, H8, D8]), ALU.add)
                    ins.then_inc(done, 1)
                elif name == "gate":
                    psl = ps[:, 0:QT * NE].rearrange("p (t e) -> p t e", t=QT)
                    if s == "A":
                        nc.vector.tensor_tensor(lg[s][:], psl, bg[:].rearrange("p (o e) -> p o e", o=1)
                                                .broadcast_to([P, QT, NE]), ALU.add).then_inc(done, 1)
                    else:
                        nc.vector.tensor_copy(lg[s][:], psl).then_inc(done, 1)
                    dve.wait_ge(*b.done(name, k))
                    link(nc.vector.tensor_reduce(nm[s][:], lg[s][:], AX.X, ALU.max, negate=True))
                    nmb = nm[s][:].rearrange("p (t o) -> p t o", o=1).broadcast_to([P, QT, NE])
                    nc.vector.tensor_tensor(lg[s][:], lg[s][:], nmb, ALU.add).then_inc(m["lg"], 1)
                    dve.wait_ge(m["eg"], b.value("eg", 1))
                    link(nc.vector.tensor_reduce(sg[s][:], eg[s][:], AX.X, ALU.add))
                    link(nc.vector.reciprocal(sg[s][:], sg[s][:]))
                    link(nc.vector.tensor_tensor(pr[s][:], eg[s][:], sg[s][:].rearrange("p (t o) -> p t o", o=1)
                                                 .broadcast_to([P, QT, NE]), ALU.mult))
                    apart(dve)
                    for t in range(QT):
                        last = nc.vector.max(top[s][:, t, :], pr[s][:, t, :])
                    link(last)
                    apart(dve)
                    for t in range(QT):
                        last = nc.vector.max_index(tix[s][:, t, :], top[s][:, t, :], pr[s][:, t, :])
                    link(last)
                    link(nc.vector.tensor_copy(tif[s][:], tix[s][:]))
                    for t in range(QT):
                        for wt_, j in ((w0, 0), (w1, 1)):
                            last = nc.vector.scalar_tensor_tensor(out=wt_[s][:, t, :], in0=iota[:], scalar=tif[s][:, t, j:j + 1],
                                                                  in1=pr[s][:, t, :], op0=ALU.is_equal, op1=ALU.mult)
                    link(last)
                    if s == "A":
                        nc.vector.tensor_tensor(w[s][:], w0[s][:], w1[s][:], ALU.add).then_inc(m["w"], 1)
                    else:
                        link(nc.vector.tensor_tensor(w[s][:], w0[s][:], w1[s][:], ALU.add))
                        link(nc.vector.tensor_reduce(ts[:], w[s][:], AX.X, ALU.add))
                        link(nc.vector.tensor_scalar(ts[:], ts[:], 1e-6, None, ALU.add))
                        link(nc.vector.reciprocal(ts[:], ts[:]))
                        link(nc.vector.tensor_tensor(w[s][:], w[s][:], ts[:].rearrange("p (t o) -> p t o", o=1)
                                                     .broadcast_to([P, QT, NE]), ALU.mult))
                        link(nc.vector.tensor_tensor(wp[:], w[s][:], pr[s][:], ALU.mult))
                        nc.vector.tensor_reduce(cb[:], wp[:], AX.X, ALU.add).then_inc(m["w"], 1)
                    return
                elif name == "wT":
                    nc.vector.tensor_copy(wT[:], ps[0:NE, 0:SEQ]).then_inc(done, 1)
                elif name == "moe":
                    t, f = divmod(k, 2)
                    dve.wait_ge(m["w"], b.value("w", 1))
                    if f == 0:
                        dve.wait_ge(m["xb2"], b.value("xb2", 0))
                    nc.vector.tensor_tensor(
                        prod[s][t][:, f * 512:(f + 1) * 512].rearrange("p (e n) -> p e n", e=4),
                        ps.rearrange("p (e n) -> p e n", e=4),
                        w[s][:, t, 4 * f:4 * f + 4].rearrange("p (e o) -> p e o", o=1).broadcast_to([P, 4, P]),
                        ALU.mult).then_inc(done, 1)
                elif name == "mx8":
                    if s == "A":
                        p, i = divmod(k, 2)
                        h = 2 * p + i
                        nc.vector.tensor_reduce(mx8[s][:, :, h], ps.rearrange("p (t n) -> p t n", t=QT), AX.X, ALU.max,
                                                negate=True).then_inc(done, 1)
                    else:
                        h, t = 2 * (k // 4) + k % 2, k // 2 % 2
                        nc.vector.tensor_reduce(mx8[s][:, t, h:h + 1], ps, AX.X, ALU.max, negate=True)\
                            .then_inc(done, 1)
                elif name == "mT8":
                    link(nc.vector.tensor_copy(m2[s][:, 0, :], ps[0:H8, 0:SEQ]))
                    nc.vector.tensor_tensor(m2[s][:, 1, :], ps[0:H8, 0:SEQ], m2[s][:, 0, :], ALU.subtract)\
                        .then_inc(done, 1)

            link_of = {"A": [0], "B": [0]}
            run(dve, step)
            assert all(link_of[s][0] == cnt[s]["vch"] for s in "AB"), link_of

        @block.gpsimd
        def _(pool):
            for (s, n), credit in CREDIT.items():
                pool.sem_inc(S[s][n], credit)
            pool.memset(ones[:], 1.0).then_inc(c_set, 1)
            pool.memset(cT["A"][:], 1.0).then_inc(c_set, 1)
            pool.memset(k8["A"][:], 1.0).then_inc(c_set, 1)
            pool.memset(k8["B"][:], 1.0).then_inc(c_set, 1)
            pool.memset(v8["A"][:], 1.0).then_inc(c_set, 1)
            pool.memset(v8["B"][:], 1.0).then_inc(c_set, 1)
            pool.memset(wo8[:], 0.0).then_inc(c_set, 1)
            pool.memset(nhalf[:], -0.5)
            pool.wait_ge(w_loaded, W_LOADS)
            pool.wait_ge(tanh_done, 1)
            for n, s in enumerate("AB"):
                pool.tensor_scalar(bo[s][:], bo[s][:], gates[:, n:n + 1], None, ALU.mult).then_inc(bias_done, 1)
            pool.wait_ge(bias_done, 2)

            def step(b, name, k, cons):
                s, m = b.s, S[b.s]
                calls = link_of[s]

                def link(ins):
                    calls[0] += 1
                    ins.then_inc(m["pch"], 1)
                    pool.wait_ge(m["pch"], b.value("pch", calls[0]))

                if name == "ln":
                    calls[0] = 0 if k == 0 else calls[0]
                    pool.wait_ge(m["mv"], b.value("mv", k + 1))
                    apart(pool)
                    link(pool.tensor_scalar(ve[s][:], mv[s][:, :, 1], EPS, None, ALU.add))
                    pool.tensor_tensor(rstd[s][:], ve[s][:], nhalf[:], ALU.pow).then_inc(m["rstd"], 1)
                    if k == 0:
                        pool.wait_ge(*b.before("sm"))
                        pool.tensor_tensor(xb[s][:], xin[s][:], bo[s][:].rearrange("p (o n) -> p o n", o=1)
                                           .broadcast_to([P, QT, P]), ALU.add).then_inc(m["xb"], 1)
                    if k == 0 and s == "A":
                        pool.wait_ge(m["ctx"], b.value("ctx", 16))
                        apart(pool)
                        pool.tensor_copy(cTb[:], cT["A"][0:CD, :]).then_inc(m["ctb"], 1)
                elif name == "qp":
                    pool.wait_ge(*b.done("qp", k))
                    apart(pool)
                    pool.tensor_copy(qAb[:, 4 * k:4 * k + 4, :], qA[0:CD, 4 * k:4 * k + 4, :]).then_inc(m["qab"], 1)
                elif name == "e":
                    pool.wait_ge(*b.done("e", k))
                    if k >= 4:
                        pool.wait_ge(m["pv"], b.value("pv", (k - 4) // 2 + 1))
                    pool.wait_ge(m["psum"], b.value("psum", k))
                    link(pool.tensor_tensor(half[:], prob[s][k][:, 0:2 * SEQ], prob[s][k][:, 2 * SEQ:], ALU.add))
                    pool.tensor_tensor(psum_k[k % 4][:], half[:, 0:SEQ], half[:, SEQ:], ALU.add).then_inc(m["psum"], 1)
                elif name == "qk":
                    pool.wait_ge(*b.done("qk"))
                    pt = parts[s]
                    apart(pool)
                    link(pool.tensor_copy(pt[:, 0, :], qk[s][:]))
                    link(pool.tensor_tensor(qk[s][:], qk[s][:], pt[:, 0, :], ALU.subtract))
                    apart(pool)
                    link(pool.tensor_copy(pt[:, 1, :], qk[s][:]))
                    pool.tensor_tensor(pt[:, 2, :], qk[s][:], pt[:, 1, :], ALU.subtract).then_inc(m["split"], 1)
                elif name == "moe" and k == 3:
                    pool.wait_ge(*b.done("moe", 3))
                    if s == "A":
                        pool.wait_ge(*b.before("sm"))
                    else:
                        pool.wait_ge(m["out"], b.value("out", 0))
                    pool.wait_ge(m["w"], b.value("w", 1))
                    for width in (4 * P, 2 * P, P):
                        for t in range(QT):
                            last = pool.tensor_tensor(prod[s][t][:, 0:width], prod[s][t][:, 0:width],
                                                      prod[s][t][:, width:2 * width], ALU.add)
                        link(last)
                    g = 2 if s == "A" else 3
                    apart(pool)
                    for t in range(QT):
                        if s == "A":
                            last = pool.tensor_scalar(prod[s][t][:, 0:P], prod[s][t][:, 0:P], gates[:, g:g + 1], None, ALU.mult)
                        else:
                            last = pool.tensor_scalar(prod[s][t][:, 0:P], prod[s][t][:, 0:P], cb[:, t:t + 1],
                                                      gates[:, g:g + 1], ALU.add, ALU.mult)
                    link(last)
                    for t in range(QT):
                        last = pool.tensor_tensor(fin[s][:, t, :], prod[s][t][:, 0:P], x1[s][:, t, :], ALU.add)
                    last.then_inc(m["xb2"], 1)
            link_of = {"A": [0], "B": [0]}
            run(pool, step)
            assert all(link_of[s][0] == cnt[s]["pch"] for s in "AB"), link_of


def kernel(**inputs):
    import concourse.bacc as bacc
    from concourse.bass_utils import run_bass_kernel_spmd

    g = {k: np.asarray(v) for k, v in inputs.items()}

    def dh(m):
        return m.reshape(m.shape[:-1] + (H8, D8)).swapaxes(-1, -2).reshape(m.shape)

    wqkv, bqkv = g["L0_ffn_W_qkv"], g["L0_ffn_b_qkv"]
    wkv, bkv = g["L1_xattn_Wkv"], g["L1_xattn_bkv"]
    sel = np.zeros((P, 4 * D8), np.float32)
    for i in range(4):
        sel[32 * i:32 * i + D8, D8 * i:D8 * i + D8] = np.eye(D8, dtype=np.float32)
    arrays = {
        "x": g["x"], "ctxT": g["ctx_768"].transpose(0, 2, 1), "g_xattn": g["g_xattn"], "g_ffn": g["g_ffn"],
        "ident": np.eye(P, dtype=np.float32), "sel": sel,
        "iota": np.tile(np.arange(NE, dtype=np.float32), (P, 1)),
        "wqT": g["L0_xattn_Wq"].reshape(P, XH, XD).transpose(2, 1, 0),
        "wkT": g["L0_xattn_Wk"].reshape(CD, XH, XD).transpose(2, 1, 0),
        "wvx": g["L0_xattn_Wv"], "wox": g["L0_xattn_Wo"].reshape(XH // 2, P, P).transpose(1, 0, 2),
        "boA": g["L0_xattn_bo"], "boB": g["L1_xattn_bo"],
        "wq8A": dh(wqkv[:, :P]), "wk8A": dh(wqkv[:, P:2 * P]), "wv8A": wqkv[:, 2 * P:],
        "bq8A": dh(bqkv[:2 * P].reshape(2, P)).T, "bv8A": bqkv[2 * P:],
        "wq8B": dh(g["L1_xattn_Wq"]), "wk8B": dh(wkv[:, :P]), "wv8B": wkv[:, P:],
        "bq8B": np.stack([dh(g["L1_xattn_bq"]), dh(bkv[:P])], axis=1), "bv8B": bkv[P:],
        "wo8": g["L1_xattn_Wo"],
        "wgA": g["L0_ffn_W_gate"], "wgB": g["L1_ffn_router_w"].T, "bg": g["L0_ffn_b_gate"],
        "weA": g["L0_ffn_W_experts"], "weB": g["L1_ffn_expert_weights"], "be": g["L0_ffn_b_experts"],
    }
    arrays = {"in_" + k: np.ascontiguousarray(v) for k, v in arrays.items()}
    nc = bacc.Bacc("TRN2", target_bir_lowering=False, num_devices=1)
    handles = {k[3:]: nc.dram_tensor(k, v.shape, mybir.dt.from_np(v.dtype), kind="ExternalInput").ap()
               for k, v in arrays.items()}
    out = nc.dram_tensor("out", (BATCH, SEQ, P), F32, kind="ExternalOutput").ap()
    build(nc, handles, out)
    r = run_bass_kernel_spmd(nc, [arrays], core_ids=[0])
    return r.results[0]["out"]
```

```python
from contextlib import ExitStack

import numpy as np
import concourse.bass as bass
from concourse import mybir

ALU = mybir.AluOpType
ACT = mybir.ActivationFunctionType
AX = mybir.AxisListType
F32 = mybir.dt.float32
BF16 = mybir.dt.bfloat16
U32 = mybir.dt.uint32

P = 128
BATCH, SEQ, KV, CD = 8, 256, 512, 96
QT = SEQ // P
XH, XD = 8, 64
H8, D8 = 16, 8
NPAIR = H8 // 2
NE = 8
KROWS = 6 * D8
MROWS = KROWS + 2
EPS = 1e-5
QPART = (0, 1, 2, 0, 1, 0)
KPART = (0, 0, 0, 1, 1, 2)

KEYS = {"F": SEQ, "B": KV}
SLOTS = {"X": 4, "F": 4, "B": 8}
WIDE = {"F": 2 * SEQ, "B": SEQ, "K": KV}


def stream_steps(s):
    t = []
    if s == "X":
        t += [("ln", 0, .4, "sm", .4, 2.5), ("qp", 0, 1.7, "st", 2.2, .3), ("qp", 1, 1.7, "st", 2.2, 0)]
        t += [("mx", k, .22, "sm", .62, .3 if k == 0 else 0) for k in range(XH * QT)]
        t += [("mT", 0, .4, "sm", .4, .3), ("vp", 0, 1.7, "st", 1.1, 0), ("vp", 1, 1.7, "st", 1.1, 0)]
        for u in range(XH):
            t.append(("e", u, 1.75, "st", 1.1, 2. if u == 0 else 0))
            if u % 2 == 0 and u > 0:
                t.append(("pv", u // 2 - 1, 2.3, "", 0, 0))
            if u % 2 == 1 and u > 1:
                t.append(("nx", u // 2 - 1, 0, "", 0, 0))
        t += [("pv", XH // 2 - 1, 2.3, "", 0, 2.5), ("nx", XH // 2 - 1, 0, "", 0, 0), ("out", 0, 1.8, "sm", .5, 2.5)]
    if s == "F":
        t += [("ln", 0, .4, "sm", .4, 2.5), ("qk", 0, .9, "st", 1.6, .3), ("sp", 0, 0, "", 0, 0), ("gate", 0, .1, "sm", .2, 0)]
        t += [("v8", 0, .5, "sm", .5, 0)]
        t += [("moe", k, .85, "sm", .65, .1) for k in range(4)]
        t += [("mx8", k, .22, "sm", .62, 2. if k == 0 else 0) for k in range(H8)]
        t += [("mT8", 0, .4, "sm", .6, .3), ("wT", 0, .4, "sm", .3, 0), ("wb", 0, .4, "sm", .3, .3)]
        for u in range(NPAIR):
            t.append(("e8", u, .45, "st", 1.1, 5. if u == 0 else 0))
            if u % 2 == 0 and u > 0:
                t.append(("pv8", u // 2 - 1, .7, "pn", 0, 0))
            if u % 2 == 1 and u > 1:
                t.append(("ev8", u // 2 - 1, 0, "", 0, 0))
        t += [("pv8", 3, .7, "pn", 0, 1.2), ("ev8", 3, 0, "", 0, .3), ("oT", 0, .8, "sm", .7, .7), ("oT", 1, .8, "sm", .7, 0)]
    if s == "K":
        t += [("cx", 0, 0, "", 0, 0), ("kk", 0, .9, "st", 1.2, 4.), ("sp", 0, 0, "", 0, 0), ("vv", 0, .5, "sm", .5, 0), ("vv", 1, .5, "sm", .5, 0)]
    if s == "B":
        t += [("ln", 0, .4, "sm", .4, 2.5), ("qk", 0, .45, "sm", .8, .3), ("sp", 0, 0, "", 0, 0)]
        t += [("mx8", k, .22, "sm", .62, 6. if k == 0 else 0) for k in range(H8 * QT)]
        t += [("mT8", 0, .4, "sm", .6, .3)]
        for u in range(2 * NPAIR):
            t.append(("e8", u, .45, "st", 1.1, 5. if u == 0 else 0))
            if u % 4 == 0 and u > 0:
                t.append(("pv8", u // 4 - 1, 1.6, "pn", 0, 0))
            if u % 4 == 2 and u > 4:
                t.append(("ev8", u // 4 - 1, 0, "", 0, 0))
        t += [("pv8", 3, 1.6, "pn", 0, 1.2), ("ev8", 3, 0, "", 0, .3), ("oT", 0, .8, "sm", .6, .7), ("oT", 1, .8, "sm", .6, 0)]
        t += [("aT", 0, .4, "sm", .4, .2), ("out8", 0, .5, "sm", .5, .2)]
        t += [("ln", 1, .4, "sm", .4, 2.5), ("gate", 0, .1, "sm", .2, .3)]
        t += [("moe", k, .85, "sm", .65, 3. if k == 0 else .1) for k in range(4)]
    return t


AFTER = {("X", "out"): ("F", "moe", 3), ("F", "oT"): ("B", "ln", 0), ("K", "kk"): ("B", "pv8", 3)}


def merge(streams):
    at = {s: 0 for s in streams}
    steps = {s: stream_steps(s) for s in streams}
    ready = {s: 0. for s in streams}
    free = {"st": [0., 0.], "sm": [0., 0.], "pn": [0., 0.]}
    pe, order, seen, held = 0., [], set(), False
    while any(at[s] < len(steps[s]) for s in streams):
        best = None
        for s in streams:
            if at[s] == len(steps[s]):
                continue
            name, k, cost, ring, took, gap = steps[s][at[s]]
            other = AFTER.get((s, name))
            if other and other[0] in streams and other not in seen:
                continue
            if name == "pv8" and held:
                continue
            start = max(pe, ready[s] + gap, free[ring][-2] if ring else 0.)
            left = sum(x[2] + x[5] for x in steps[s][at[s]:])
            if best is None or (start, -left) < best[:2]:
                best = (start, -left, s)
        start, _, s = best
        name, k, cost, ring, took, gap = steps[s][at[s]]
        at[s] += 1
        seen.add((s, name, k))
        held = name == "pv8" or held and name != "ev8"
        pe = start + cost
        ready[s] = pe
        if ring:
            free[ring].append(max(free[ring][-1], pe) + took)
            if at[s] < len(steps[s]) and steps[s][at[s]][5] > 0:
                ready[s] = free[ring][-1]
        order.append((s, name, k, ring))
    return order


ORDER = {streams: merge(streams) for streams in ("X", "XFK", "XFKB", "FKB", "B")}
RINGS = {s: {r: sum(step[3] == r for step in ORDER[s]) for r in ("st", "sm", "pn")} for s in ORDER}

COUNTS = {
    "X": dict(xin=16, ctx=16, mv=1, rstd=1, xh=1, xb=1, ctb=1, mroww=16, mrowr=16, psum=XH, pv=XH // 2, norm=XH // 2,
              pch=9, vch=5),
    "F": dict(mv=1, rstd=1, xh=1, split=1, splitw=16, qks=18 * 16, lg=1, eg=1, w=1, used=4, fin=1, m2w=16, m2r=32,
              xm=2, pch=8, vch=14),
    "K": dict(ctx=16, split=1, splitw=16, qks=12 * 16, vch=2),
    "B": dict(mv=2, rstd=2, xh=2, xb=1, split=1, splitw=16, qks=6 * 16, lg=1, eg=1, w=1, used=4, fin=1, m2w=16, m2r=32,
              out=16, pch=9, vch=21),
}
CREDIT = {("B", "used"): 2, ("F", "used"): 2, ("B", "out"): 16}


def build(nc, a, out):
    ctx = ExitStack()
    with ctx:
        def sb(name, shape, dt=F32):
            return ctx.enter_context(nc.sbuf_tensor(name, shape, dt))

        def dram(name, shape, dt):
            return nc.dram_tensor(name, shape, dt, kind="Internal").ap()

        def sem(name):
            return ctx.enter_context(nc.semaphore(name))

        ident = sb("ident", [P, P])
        iota = sb("iota", [P, NE])
        ones = sb("ones", [P, XD])
        wqk = sb("wqk", [P, XH, CD])
        wvx = sb("wvx", [CD, XH * XD])
        wox = sb("wox", [P, XH // 2, P])
        gates = sb("gates", [P, 4])
        graw = sb("graw", [P, 4])
        bo = {s: sb("bo" + s, [P, P]) for s in "XB"}
        wq8 = {s: sb("wq8" + s, [P, P]) for s in "FB"}
        wk8 = {"F": sb("wk8F", [P, P]), "B": sb("wk8B", [CD, P])}
        wv8 = {"F": sb("wv8F", [P, P]), "B": sb("wv8B", [CD, P])}
        bq8 = {s: sb("bq8" + s, [P, 2]) for s in "FB"}
        bv8 = {s: sb("bv8" + s, [P, P]) for s in "FB"}
        wo8 = sb("wo8", [P, P])
        wg = {s: sb("wg" + s, [P, NE]) for s in "FB"}
        bg = sb("bg", [P, NE])
        we = {s: sb("we" + s, [P, NE * P]) for s in "FB"}
        be = sb("be", [NE, P])
        nhalf = sb("nhalf", [P, QT])

        def per(streams, name, shape, dt=F32):
            return {s: sb(name + s, shape, dt) for s in streams}

        xin = sb("xin", [P, QT, P])
        x1 = {"F": sb("x1", [P, QT, P]), "B": sb("x3", [P, QT, P])}
        xmid = sb("xmid", [P, QT, P])
        source = {("X", 0): xin, ("F", 0): x1["F"], ("B", 0): xmid, ("B", 1): x1["B"]}
        cT = per("XK", "cT", [CD + 1, KV])
        xb = per("XB", "xb", [P, QT, P])
        st6 = per("XFB", "st6", [P, QT, 6])
        mv = per("XFB", "mv", [P, QT, 2])
        ve = per("XFB", "ve", [P, QT])
        rstd = per("XFB", "rstd", [P, QT])
        xh = per("XFB", "xh", [P, QT, P])
        xT = per("XFB", "xT", [P, SEQ])
        qA = sb("qA", [CD + 1, XH, SEQ])
        qAb = sb("qAb", [CD, XH, SEQ], BF16)
        cTb = sb("cTb", [CD, KV], BF16)
        vX = sb("vX", [P, KV // P, XH * XD])
        mxA = sb("mxA", [P, QT, XH])
        mrow = sb("mrow", [XH, SEQ])
        prob = {s: [sb(f"prob{s}{n}", [P, 4 * SEQ]) for n in range(SLOTS[s])] for s in "XFB"}
        wqT = prob["X"][0][0:XD, 0:XH * P].rearrange("p (h n) -> p h n", h=XH)
        wkT = prob["X"][1][0:XD, 0:XH * CD].rearrange("p (h n) -> p h n", h=XH)
        half = sb("half", [P, 2 * SEQ])
        psum_k = [sb(f"psum_k{n}", [P, SEQ]) for n in range(4)]
        rden = sb("rden", [P, SEQ])
        oTX = sb("oTX", [P, XH // 2, SEQ])
        qk = {s: sb("qk" + s, [P, WIDE[s]]) for s in "FKB"}
        parts = {s: sb("parts" + s, [P, 3, WIDE[s]], BF16) for s in "FKB"}
        q8 = {s: sb("q8" + s, [P, NPAIR, SEQ], BF16) for s in "FB"}
        k8 = {s: sb("k8" + s, [P, NPAIR, KEYS[s]], BF16) for s in "FB"}
        v8 = {s: sb("v8" + s, [P, KEYS[s] // P, H8, 32]) for s in "FB"}
        mx8 = per("FB", "mx8", [P, QT, H8])
        m2 = per("FB", "m2", [H8, 2, SEQ], BF16)
        oU = per("FB", "oU", [P, 4, SEQ])
        rr = per("FB", "rr", [P, QT, H8])
        att = per("FB", "att", [P, QT, P])
        attT = xT["B"]
        lg = per("FB", "lg", [P, QT, NE])
        nm = per("FB", "nm", [P, QT])
        eg = per("FB", "eg", [P, QT, NE])
        sg = per("FB", "sg", [P, QT])
        pr = per("FB", "pr", [P, QT, NE])
        top = per("FB", "top", [P, QT, 8])
        tix = per("FB", "tix", [P, QT, 8], U32)
        tif = per("FB", "tif", [P, QT, 8])
        w0 = per("FB", "w0", [P, QT, NE])
        w1 = per("FB", "w1", [P, QT, NE])
        w = per("FB", "w", [P, QT, NE])
        ts = sb("ts", [P, QT])
        wp = sb("wp", [P, QT, NE])
        cb = sb("cb", [P, QT])
        wT = sb("wT", [NE, SEQ])
        prod = {s: [sb(f"prod{s}{n}", [P, 4 * P]) for n in range(2)] for s in "FB"}
        acc = per("FB", "acc", [P, QT, P])
        fin = per("FB", "fin", [P, QT, P])

        mrow_d = dram("mrow_d", [XH, SEQ], F32)
        part_d = {s: dram("part_d" + s, [3, P, WIDE[s]], BF16) for s in "FKB"}
        m2_d = {s: dram("m2_d" + s, [2, H8, SEQ], BF16) for s in "FB"}

        st = ctx.enter_context(nc.psum_tensor("st", [P, 2, 1024], F32))
        sm = ctx.enter_context(nc.psum_tensor("sm", [P, 2, 512], F32))
        pvx = ctx.enter_context(nc.psum_tensor("pvx", [P, 512], F32))
        pv8 = ctx.enter_context(nc.psum_tensor("pv8", [P, 512], F32))

        ring_full = {r: sem(r + "_full") for r in ("st", "sm", "pn")}
        ring_done = {r: sem(r + "_done") for r in ("st", "sm", "pn")}
        ring_psum = {"st": st, "sm": sm}
        S = {s: {n: sem(n + s) for n in COUNTS[s]} for s in "XFKB"}
        cnt = COUNTS
        w_loaded, c_set, tanh_done, bias_done = sem("w_loaded"), sem("c_set"), sem("tanh_done"), sem("bias_done")
        passed = sem("passed")
        fold_ps, fold_ev = sem("fold_ps"), sem("fold_ev")

        class Stream:

            def __init__(self, s, batch, base, places):
                self.s, self.batch, self.base, self.places = s, batch, base, places

            def value(self, n, k):
                return self.batch * COUNTS[self.s][n] + (k + CREDIT.get((self.s, n), 0))

            def place(self, name, k):
                ring, n = self.places[self.s, name, k]
                reg, const = self.base[ring]
                return ring, reg, const + n

            def slot(self, name, k):
                ring, _, n = self.place(name, k)
                return ring_psum[ring][:, n % 2, :] if ring != "pn" else pv8[:]

            def full(self, name, k):
                ring, reg, n = self.place(name, k)
                return ring_full[ring], reg + (n + 1)

            def done(self, name, k=0):
                ring, reg, n = self.place(name, k)
                return ring_done[ring], reg + (n + 1)

            def before(self, ring):
                reg, const = self.base[ring]
                return ring_done[ring], reg + const

        def run(eng, step):
            def steps(streams, batch, base):
                places, n = {}, {r: 0 for r in base}
                for s, name, k, ring in ORDER[streams]:
                    if ring:
                        places[s, name, k] = (ring, n[ring])
                        n[ring] += 1
                at = {s: Stream(s, batch[s], base, places) for s in streams}
                for s, name, k, ring in ORDER[streams]:
                    step(at[s], name, k, ring)

            def start(done, reg=0):
                return {r: (reg * RINGS["XFKB"][r], sum(RINGS[x][r] for x in done)) for r in ("st", "sm", "pn")}

            full = BATCH - 2
            assert all(RINGS["XFKB"][r] % 2 == 0 for r in ("st", "sm"))
            steps("X", dict(X=0), start([]))
            steps("XFK", dict(X=1, F=0, K=0), start(["X"]))
            with eng.Fori(0, full) as i:
                steps("XFKB", dict(X=i + 2, F=i + 1, K=i + 1, B=i), start(["X", "XFK"], i))
            steps("FKB", dict(F=BATCH - 1, K=BATCH - 1, B=BATCH - 2), start(["X", "XFK"] + ["XFKB"] * full))
            steps("B", dict(B=BATCH - 1), start(["X", "XFK"] + ["XFKB"] * full + ["FKB"]))

        NC = {s: KEYS[s] // P for s in "FB"}
        block = ctx.enter_context(nc.Block())

        def apart(eng):
            eng.sem_inc(passed, 1)

        W_LOADS = 0
        loads = [(ident[:], a["ident"]), (wqT, a["wqT"]), (wkT, a["wkT"]),
                 (graw[:, 0:2], a["g_xattn"].rearrange("(o n) -> o n", o=1).broadcast_to([P, 2])),
                 (graw[:, 2:4], a["g_ffn"].rearrange("(o n) -> o n", o=1).broadcast_to([P, 2])),
                 (wo8[:], a["wo8"]), (iota[:], a["iota"]), (wvx[:], a["wvx"]), (wox[:], a["wox"]),
                 (be[:], a["be"]), (bg[:], a["bg"].rearrange("(o n) -> o n", o=1).broadcast_to([P, NE]))]
        loads += [(bo[s][:], a["bo" + s].rearrange("(o n) -> o n", o=1).broadcast_to([P, P])) for s in "XB"]
        for s in "FB":
            loads += [(wq8[s][:], a["wq8" + s]), (wk8[s][:], a["wk8" + s]), (wv8[s][:], a["wv8" + s]),
                      (bq8[s][:], a["bq8" + s]),
                      (bv8[s][:], a["bv8" + s].rearrange("(o n) -> o n", o=1).broadcast_to([P, P])),
                      (wg[s][:], a["wg" + s]),
                      (we[s][:].rearrange("p (e n) -> p e n", e=NE), a["we" + s].rearrange("e k n -> k e n"))]
        W_LOADS = 16 * len(loads)
        MEMSETS = 7

        @block.sync
        def _(sp):
            def load_x(batch):
                sp.dma_start(xin[:], a["x"][bass.ds(batch, 1)].rearrange("o (t p) n -> p (o t) n", p=P))\
                    .then_inc(S["X"]["xin"], 16)

            def load_ctx(s, batch):
                sp.dma_start(cT[s][0:CD], a["ctxT"][bass.ds(batch, 1)].rearrange("o c t -> (o c) t"))\
                    .then_inc(S[s]["ctx"], 16)

            load_x(0)
            for dst, src in loads:
                sp.dma_start(dst, src).then_inc(w_loaded, 16)
            sp.wait_ge(c_set, MEMSETS)
            load_ctx("X", 0)

            def step(b, name, k, ring):
                s, m = b.s, S[b.s]
                if (s, name) == ("X", "mT"):
                    sp.wait_ge(*b.done("mT"))
                    sp.dma_start(mrow_d, mrow[:]).then_inc(m["mroww"], 16)
                    sp.wait_ge(m["mroww"], b.value("mroww", 16))
                    sp.dma_start(qA[CD:CD + 1], mrow_d.rearrange("(o h) n -> o h n", o=1)).then_inc(m["mrowr"], 16)
                if (s, name) == ("X", "out"):
                    sp.wait_ge(*b.done("out"))
                    load_x((b.batch + 1) % BATCH)
                    load_ctx("X", (b.batch + 1) % BATCH)
                if name == "cx":
                    sp.wait_ge(*b.before("sm"))
                    sp.wait_ge(*b.before("st"))
                    load_ctx("K", b.batch)
                if name == "sp":
                    sp.wait_ge(m["split"], b.value("split", 1))
                    sp.dma_start(part_d[s].rearrange("t p n -> p t n"), parts[s][:]).then_inc(m["splitw"], 16)
                    sp.wait_ge(m["splitw"], b.value("splitw", 16))
                    src = part_d[s].rearrange("t (d p i) n -> i (t d) p n", i=2, p=NPAIR)
                    for i in range(2):
                        if s != "K":
                            for j0, n in ((0, 3), (3, 2), (5, 1)):
                                r = 64 * i + D8 * j0
                                sp.dma_start(q8[s][r:r + D8 * n], src[i, 0:D8 * n, :, 0:SEQ]).then_inc(m["qks"], 16)
                        if s != "B":
                            for j in range(6):
                                r, t = 64 * i + D8 * j, D8 * KPART[j]
                                keys = k8["F" if s == "F" else "B"]
                                sp.dma_start(keys[r:r + D8], src[i, t:t + D8, :, SEQ * (s == "F"):])\
                                    .then_inc(m["qks"], 16)
                if name == "mT8":
                    sp.wait_ge(*b.done("mT8"))
                    sp.dma_start(m2_d[s].rearrange("t h n -> h t n"), m2[s][:]).then_inc(m["m2w"], 16)
                    sp.wait_ge(m["m2w"], b.value("m2w", 16))
                    for i in range(2):
                        sp.dma_start(q8[s][64 * i + KROWS:64 * i + MROWS],
                                     m2_d[s].rearrange("t (p i) n -> i t p n", i=2)[i]).then_inc(m["m2r"], 16)
                if (s, name, k) == ("B", "moe", 3):
                    sp.wait_ge(m["fin"], b.value("fin", 1))
                    sp.dma_start(out[bass.ds(b.batch, 1)].rearrange("o (t p) n -> p (o t) n", p=P), fin["B"][:])\
                        .then_inc(m["out"], 16)
            run(sp, step)
            sp.wait_ge(S["B"]["out"], 16 * BATCH + CREDIT["B", "out"])
            sp.wait_ge(S["X"]["xin"], 16 * (BATCH + 1))

        @block.tensor
        def _(pe):
            pe.wait_ge(w_loaded, W_LOADS)
            pe.wait_ge(c_set, MEMSETS)
            for h in range(XH):
                fold = nc.tensor.matmul(st[:, h // 4, (h % 4) * P:(h % 4) * P + CD], wqT[:, h, :], wkT[:, h, :],
                                        start=True, stop=True)
            fold.then_inc(fold_ps, 1)
            pe.wait_ge(fold_ev, 2)

            def step(b, name, k, ring):
                s, m = b.s, S[b.s]
                if ring:
                    _, reg, n = b.place(name, k)
                    depth = 1 if ring == "pn" else 2
                    if not isinstance(reg, int) or n >= depth:
                        pe.wait_ge(ring_done[ring], reg + (n + 1 - depth))
                    ps = b.slot(name, k)
                mm, last = nc.tensor.matmul, None
                if name == "ln":
                    pe.wait_ge(m["xh"], b.value("xh", k + 1))
                    for t in range(QT):
                        last = nc.tensor.transpose(ps[:, t * P:(t + 1) * P], xh[s][:, t, :], ident[:])
                elif name == "qp":
                    pe.wait_ge(*b.done("ln"))
                    for j in range(4):
                        last = mm(ps[0:CD, j * SEQ:(j + 1) * SEQ], wqk[:, 4 * k + j, :], xT[s][:], start=True, stop=True)
                elif name == "vp":
                    pe.wait_ge(m["ctx"], b.value("ctx", 16))
                    for j in range(2):
                        c = 2 * k + j
                        last = mm(ps[:, j * 512:(j + 1) * 512], cT["X"][0:CD, c * P:(c + 1) * P], wvx[:],
                                  start=True, stop=True)
                elif name == "mx":
                    h, t = divmod(k, QT)
                    pe.wait_ge(*b.done("qp", h // 4))
                    pe.wait_ge(m["ctb"], b.value("ctb", 1))
                    last = mm(ps, qAb[:, h, t * P:(t + 1) * P], cTb[:], start=True, stop=True)
                elif name == "mT":
                    pe.wait_ge(*b.done("mx", XH * QT - 1))
                    for t in range(QT):
                        last = nc.tensor.transpose(ps[0:XH, t * P:(t + 1) * P], mxA[:, t, :], ident[:])
                elif name == "e":
                    pe.wait_ge(m["mrowr"], b.value("mrowr", 16))
                    for c in range(KV // P):
                        last = mm(ps[:, c * SEQ:(c + 1) * SEQ], cT["X"][:, c * P:(c + 1) * P], qA[:, k, :],
                                  start=True, stop=True)
                elif name == "pv":
                    pe.wait_ge(*b.done("e", 2 * k + 1))
                    pe.wait_ge(*b.done("vp", 1))
                    if k > 0:
                        pe.wait_ge(m["norm"], b.value("norm", k))
                    for c in range(KV // P):
                        for i in range(2):
                            h = 2 * k + i
                            mm(pvx[64 * i:64 * i + 64, 0:SEQ], vX[:, c, h * XD:(h + 1) * XD],
                               prob[s][h % SLOTS[s]][:, c * SEQ:(c + 1) * SEQ], start=(c == 0), stop=(c == KV // P - 1))
                    pe.wait_ge(m["psum"], b.value("psum", 2 * k + 2))
                    for i in range(2):
                        ins = mm(pvx[64 * i:64 * i + 64, SEQ:2 * SEQ], ones[:], psum_k[(2 * k + i) % 4][:],
                                 start=True, stop=True)
                    ins.then_inc(m["pv"], 1)
                elif name == "out":
                    pe.wait_ge(m["norm"], b.value("norm", XH // 2))
                    for t in range(QT):
                        for j in range(XH // 2):
                            last = mm(ps[:, t * P:(t + 1) * P], oTX[:, j, t * P:(t + 1) * P], wox[:, j, :],
                                      start=(j == 0), stop=(j == XH // 2 - 1))
                elif name == "qk":
                    pe.wait_ge(*b.done("ln"))
                    last = mm(ps[:, 0:SEQ], wq8[s][:], xT[s][:], start=True, stop=True)
                    if s == "F":
                        last = mm(ps[:, 512:512 + SEQ], wk8[s][:], xT[s][:], start=True, stop=True)
                elif name == "kk":
                    pe.wait_ge(m["ctx"], b.value("ctx", 16))
                    last = mm(ps[:, 0:KV], wk8["B"][:], cT["K"][0:CD, :], start=True, stop=True)
                elif name in ("v8", "vv"):
                    if s == "F":
                        pe.wait_ge(*b.done("ln"))
                    for j in range(2):
                        c = 2 * k + j
                        tok = xT["F"][:, c * P:(c + 1) * P] if s == "F" else cT["K"][0:CD, c * P:(c + 1) * P]
                        last = mm(ps[:, j * P:(j + 1) * P], tok, wv8["F" if s == "F" else "B"][:], start=True, stop=True)
                elif name == "gate":
                    pe.wait_ge(*b.done("ln", 0 if s == "F" else 1))
                    for t in range(QT):
                        last = mm(ps[:, t * NE:(t + 1) * NE], xT[s][:, t * P:(t + 1) * P], wg[s][:], start=True, stop=True)
                elif name == "moe":
                    t, f = divmod(k, 2)
                    last = mm(ps, xT[s][:, t * P:(t + 1) * P], we[s][:, f * 512:(f + 1) * 512], start=True, stop=True)
                elif name == "mx8":
                    pe.wait_ge(m["qks"], b.value("qks", COUNTS[s]["qks"]))
                    if s == "F":
                        p, i = divmod(k, 2)
                        for t in range(QT):
                            last = mm(ps[:, t * SEQ:(t + 1) * SEQ], q8[s][64 * i:64 * i + KROWS, p, t * P:(t + 1) * P],
                                      k8[s][64 * i:64 * i + KROWS, p, :], start=True, stop=True)
                    else:
                        if k == 0:
                            pe.wait_ge(S["K"]["qks"], (b.batch + 1) * COUNTS["K"]["qks"])
                        p, t, i = k // 4, k // 2 % 2, k % 2
                        last = mm(ps, q8[s][64 * i:64 * i + KROWS, p, t * P:(t + 1) * P],
                                  k8[s][64 * i:64 * i + KROWS, p, :], start=True, stop=True)
                elif name == "mT8":
                    pe.wait_ge(*b.done("mx8", H8 * NC[s] // 2 - 1))
                    for t in range(QT):
                        last = nc.tensor.transpose(ps[0:H8, t * P:(t + 1) * P], mx8[s][:, t, :], ident[:])
                elif name == "wT":
                    pe.wait_ge(m["w"], b.value("w", 1))
                    for t in range(QT):
                        last = nc.tensor.transpose(ps[0:NE, t * P:(t + 1) * P], w[s][:, t, :], ident[:])
                elif name == "wb":
                    pe.wait_ge(*b.done("wT"))
                    for t in range(QT):
                        last = mm(ps[:, t * P:(t + 1) * P], wT[:, t * P:(t + 1) * P], be[:], start=True, stop=True)
                elif name == "e8":
                    pe.wait_ge(m["m2r"], b.value("m2r", 32))
                    p, c0 = (k, 0) if s == "F" else (k // 2, 2 * (k % 2))
                    for c in range(2):
                        for i in range(2):
                            last = mm(ps[:, 512 * i + SEQ * c:512 * i + SEQ * (c + 1)],
                                      k8[s][64 * i:64 * i + MROWS, p, (c0 + c) * P:(c0 + c + 1) * P],
                                      q8[s][64 * i:64 * i + MROWS, p, :], start=True, stop=True)
                elif name == "pv8":
                    n = NC[s]
                    pe.wait_ge(*b.done("e8", n * (k + 1) - 1))
                    pe.wait_ge(*(b.done("v8") if s == "F" else b.before("sm")))
                    for c in range(n):
                        for i in range(4):
                            h = 4 * k + i
                            u = (h // 2) * (n // 2) + c // 2
                            o = 512 * (h % 2) + SEQ * (c % 2)
                            last = mm(ps[32 * i:32 * i + 32, 0:SEQ], v8[s][:, c, h, :], prob[s][u % SLOTS[s]][:, o:o + SEQ],
                                     start=(c == 0), stop=(c == n - 1), tile_position=(0, 32 * i))
                elif name == "oT":
                    pe.wait_ge(*b.done("pv8", 3))
                    for g in range(4):
                        last = nc.tensor.transpose(ps[:, g * P:(g + 1) * P], oU[s][:, g, k * P:(k + 1) * P], ident[:])
                elif name == "aT":
                    pe.wait_ge(*b.done("oT", 1))
                    for t in range(QT):
                        last = nc.tensor.transpose(ps[:, t * P:(t + 1) * P], att[s][:, t, :], ident[:])
                elif name == "out8":
                    pe.wait_ge(*b.done("aT"))
                    for t in range(QT):
                        last = mm(ps[:, t * P:(t + 1) * P], attT[:, t * P:(t + 1) * P], wo8[:], start=True, stop=True)
                if ring:
                    last.then_inc(ring_full[ring], 1)
            run(pe, step)

        @block.scalar
        def _(act):
            act.wait_ge(w_loaded, W_LOADS)
            nc.scalar.activation(gates[:], graw[:], ACT.Tanh).then_inc(tanh_done, 1)
            act.wait_ge(fold_ps, 1)
            for j in range(2):
                nc.scalar.activation(wqk[:, 4 * j:4 * j + 4, :],
                                     st[:, j, 0:4 * P].rearrange("p (h n) -> p h n", h=4)[:, :, 0:CD],
                                     ACT.Copy).then_inc(fold_ev, 1)

            def step(b, name, k, ring):
                s, m = b.s, S[b.s]
                if (s, name) == ("X", "ln"):
                    act.wait_ge(m["ctx"], b.value("ctx", 16))
                    nc.scalar.activation(cTb[:], cT["X"][0:CD, :], ACT.Copy).then_inc(m["ctb"], 1)
                if name == "gate":
                    act.wait_ge(m["lg"], b.value("lg", 1))
                    nc.scalar.activation(eg[s][:], lg[s][:], ACT.Exp).then_inc(m["eg"], 1)
                if name == "ev8":
                    act.wait_ge(*b.full("pv8", k))
                    nc.scalar.activation(oU[s][:, k, :], pv8[:, 0:SEQ], ACT.Copy).then_inc(ring_done["pn"], 1)
                if ring != "st":
                    return
                act.wait_ge(*b.full(name, k))
                ps = b.slot(name, k)
                done = ring_done["st"]
                if name == "qp":
                    heads = ps[0:CD].rearrange("p (h n) -> p h n", h=4)
                    nc.scalar.activation(qAb[:, 4 * k:4 * k + 4, :], heads, ACT.Copy)
                    nc.scalar.activation(qA[0:CD, 4 * k:4 * k + 4, :], heads, ACT.Copy).then_inc(done, 1)
                elif name == "vp":
                    nc.scalar.activation(vX[:, 2 * k:2 * k + 2, :], ps.rearrange("p (h n) -> p h n", h=2),
                                         ACT.Copy).then_inc(done, 1)
                elif name == "e":
                    if k >= SLOTS[s]:
                        act.wait_ge(m["pv"], b.value("pv", (k - SLOTS[s]) // 2 + 1))
                    nc.scalar.activation(prob[s][k % SLOTS[s]][:], ps, ACT.Exp, scale=float(XD) ** -0.5).then_inc(done, 1)
                elif name in ("qk", "kk"):
                    where = {"F": [(0, 0, SEQ, 0), (SEQ, 512, SEQ, 1)], "K": [(0, 0, KV, 1)]}[s]
                    for to, at, n, j in where:
                        bias = bq8["B" if s == "K" else s][:, j:j + 1]
                        nc.scalar.activation(parts[s][:, 0, to:to + n], ps[:, at:at + n], ACT.Identity, bias=bias)
                        last = nc.scalar.activation(qk[s][:, to:to + n], ps[:, at:at + n], ACT.Identity, bias=bias)
                    last.then_inc(done, 1)
                elif name == "e8":
                    if k >= SLOTS[s]:
                        act.wait_ge(*b.full("pv8", (k - SLOTS[s]) // NC[s]))
                    nc.scalar.activation(prob[s][k % SLOTS[s]][:], ps, ACT.Exp, scale=float(D8) ** -0.5).then_inc(done, 1)
            run(act, step)
        @block.vector
        def _(dve):
            dve.wait_ge(w_loaded, W_LOADS)

            def step(b, name, k, ring):
                s, m = b.s, S[b.s]
                calls = link_of[s]
                if k == 0 and name in ("ln", "kk") :
                    calls[0] = 0

                def link(ins):
                    calls[0] += 1
                    ins.then_inc(m["vch"], 1)
                    dve.wait_ge(m["vch"], b.value("vch", calls[0]))

                if name == "ln":
                    src = source[s, k]
                    if s == "X":
                        dve.wait_ge(m["xin"], b.value("xin", 16))
                    elif s == "F":
                        dve.wait_ge(*b.before("sm"))
                    elif k == 0:
                        dve.wait_ge(S["F"]["xm"], (b.batch + 1) * COUNTS["F"]["xm"])
                    else:
                        dve.wait_ge(*b.done("out8"))
                    for t in range(QT):
                        last = nc.vector.bn_stats(st6[s][:, t, :], src[:, t, :])
                    link(last)
                    apart(dve)
                    for t in range(QT):
                        last = nc.vector.bn_aggr(mv[s][:, t, :], st6[s][:, t, :])
                    last.then_inc(m["mv"], 1)
                    dve.wait_ge(m["rstd"], b.value("rstd", k + 1))
                    for t in range(QT):
                        last = nc.vector.tensor_scalar(xh[s][:, t, :], src[:, t, :], mv[s][:, t, 0:1], rstd[s][:, t:t + 1],
                                                       ALU.subtract, ALU.mult)
                    last.then_inc(m["xh"], 1)
                if name == "nx":
                    dve.wait_ge(m["pv"], b.value("pv", k + 1))
                    link(nc.vector.reciprocal(rden[:], pvx[:, SEQ:2 * SEQ]))
                    nc.vector.tensor_tensor(oTX[:, k, :], pvx[:, 0:SEQ], rden[:], ALU.mult).then_inc(m["norm"], 1)
                if name == "sp":
                    dve.wait_ge(*b.done("kk" if s == "K" else "qk"))
                    link(nc.vector.tensor_tensor(qk[s][:], qk[s][:], parts[s][:, 0, :], ALU.subtract))
                    link(nc.vector.tensor_copy(parts[s][:, 1, :], qk[s][:]))
                    nc.vector.tensor_tensor(parts[s][:, 2, :], qk[s][:], parts[s][:, 1, :], ALU.subtract)\
                        .then_inc(m["split"], 1)
                if ring != "sm":
                    return
                dve.wait_ge(*b.full(name, k))
                ps = b.slot(name, k)
                done = ring_done["sm"]
                tiles = ps[:, 0:QT * P].rearrange("p (t n) -> p t n", t=QT)
                if name == "ln":
                    nc.vector.tensor_copy(xT[s][:], ps[:, 0:SEQ]).then_inc(done, 1)
                elif name == "qk":
                    nc.vector.tensor_scalar(parts[s][:, 0, :], ps[:, 0:SEQ], bq8[s][:, 0:1], None, ALU.add)
                    nc.vector.tensor_scalar(qk[s][:], ps[:, 0:SEQ], bq8[s][:, 0:1], None, ALU.add).then_inc(done, 1)
                elif name == "mx":
                    h, t = divmod(k, QT)
                    nc.vector.tensor_reduce(mxA[:, t, h:h + 1], ps, AX.X, ALU.max, negate=True).then_inc(done, 1)
                elif name == "mT":
                    nc.vector.tensor_copy(mrow[:], ps[0:XH, 0:SEQ]).then_inc(done, 1)
                elif name in ("out", "out8"):
                    dve.wait_ge(m["xb"], b.value("xb", 1))
                    if s == "X":
                        dve.wait_ge(S["F"]["fin"], b.batch)
                    nc.vector.scalar_tensor_tensor(out=x1["F" if s == "X" else "B"][:], in0=tiles,
                                                   scalar=gates[:, 0:1] if s == "X" else gates[:, 1:2], in1=xb[s][:],
                                                   op0=ALU.mult, op1=ALU.add).then_inc(done, 1)
                elif name == "wb":
                    dve.wait_ge(m["fin"], b.value("fin", 1))
                    nc.vector.scalar_tensor_tensor(out=fin[s][:], in0=tiles, scalar=gates[:, 2:3], in1=fin[s][:],
                                                   op0=ALU.mult, op1=ALU.add).then_inc(done, 1)
                elif name == "oT":
                    heads = ps.rearrange("p (h n) -> p h n", h=H8)
                    link(nc.vector.reciprocal(rr[s][:, k, :], heads[:, :, D8]))
                    nc.vector.tensor_tensor(att[s][:, k, :].rearrange("p (h d) -> p h d", h=H8), heads[:, :, 0:D8],
                                            rr[s][:, k, :].rearrange("p (h o) -> p h o", o=1).broadcast_to([P, H8, D8]),
                                            ALU.mult).then_inc(done, 1)
                    if s == "F":
                        dve.wait_ge(*b.done("oT", k))
                        if k == 0:
                            dve.wait_ge(S["B"]["xb"], b.batch)
                        nc.vector.scalar_tensor_tensor(out=xmid[:, k, :], in0=att[s][:, k, :], scalar=gates[:, 2:3],
                                                       in1=fin["F"][:, k, :], op0=ALU.mult, op1=ALU.add).then_inc(m["xm"], 1)
                elif name == "aT":
                    nc.vector.tensor_copy(attT[:], ps[:, 0:SEQ]).then_inc(done, 1)
                elif name in ("v8", "vv"):
                    to = "F" if s == "F" else "B"
                    nc.vector.tensor_tensor(
                        v8[to][:, 2 * k:2 * k + 2, :, 0:D8],
                        ps[:, 0:2 * P].rearrange("p (c h d) -> p c h d", c=2, h=H8),
                        bv8[to][:].rearrange("p (o h d) -> p o h d", o=1, h=H8).broadcast_to([P, 2, H8, D8]),
                        ALU.add).then_inc(done, 1)
                elif name == "gate":
                    psl = ps[:, 0:QT * NE].rearrange("p (t e) -> p t e", t=QT)
                    if s == "F":
                        nc.vector.tensor_tensor(lg[s][:], psl, bg[:].rearrange("p (o e) -> p o e", o=1)
                                                .broadcast_to([P, QT, NE]), ALU.add).then_inc(done, 1)
                    else:
                        nc.vector.tensor_copy(lg[s][:], psl).then_inc(done, 1)
                    dve.wait_ge(*b.done(name, k))
                    link(nc.vector.tensor_reduce(nm[s][:], lg[s][:], AX.X, ALU.max, negate=True))
                    nmb = nm[s][:].rearrange("p (t o) -> p t o", o=1).broadcast_to([P, QT, NE])
                    nc.vector.tensor_tensor(lg[s][:], lg[s][:], nmb, ALU.add).then_inc(m["lg"], 1)
                    dve.wait_ge(m["eg"], b.value("eg", 1))
                    link(nc.vector.tensor_reduce(sg[s][:], eg[s][:], AX.X, ALU.add))
                    link(nc.vector.reciprocal(sg[s][:], sg[s][:]))
                    link(nc.vector.tensor_tensor(pr[s][:], eg[s][:], sg[s][:].rearrange("p (t o) -> p t o", o=1)
                                                 .broadcast_to([P, QT, NE]), ALU.mult))
                    apart(dve)
                    for t in range(QT):
                        last = nc.vector.max(top[s][:, t, :], pr[s][:, t, :])
                    link(last)
                    apart(dve)
                    for t in range(QT):
                        last = nc.vector.max_index(tix[s][:, t, :], top[s][:, t, :], pr[s][:, t, :])
                    link(last)
                    link(nc.vector.tensor_copy(tif[s][:], tix[s][:]))
                    for t in range(QT):
                        for wt_, j in ((w0, 0), (w1, 1)):
                            last = nc.vector.scalar_tensor_tensor(out=wt_[s][:, t, :], in0=iota[:], scalar=tif[s][:, t, j:j + 1],
                                                                  in1=pr[s][:, t, :], op0=ALU.is_equal, op1=ALU.mult)
                    link(last)
                    if s == "F":
                        nc.vector.tensor_tensor(w[s][:], w0[s][:], w1[s][:], ALU.add).then_inc(m["w"], 1)
                    else:
                        link(nc.vector.tensor_tensor(w[s][:], w0[s][:], w1[s][:], ALU.add))
                        link(nc.vector.tensor_reduce(ts[:], w[s][:], AX.X, ALU.add))
                        link(nc.vector.tensor_scalar(ts[:], ts[:], 1e-6, None, ALU.add))
                        link(nc.vector.reciprocal(ts[:], ts[:]))
                        link(nc.vector.tensor_tensor(w[s][:], w[s][:], ts[:].rearrange("p (t o) -> p t o", o=1)
                                                     .broadcast_to([P, QT, NE]), ALU.mult))
                        link(nc.vector.tensor_tensor(wp[:], w[s][:], pr[s][:], ALU.mult))
                        nc.vector.tensor_reduce(cb[:], wp[:], AX.X, ALU.add).then_inc(m["w"], 1)
                elif name == "wT":
                    nc.vector.tensor_copy(wT[:], ps[0:NE, 0:SEQ]).then_inc(done, 1)
                elif name == "moe":
                    t, f = divmod(k, 2)
                    dve.wait_ge(m["w"], b.value("w", 1))
                    dve.wait_ge(m["used"], b.value("used", k - 1))
                    nc.vector.tensor_tensor(
                        prod[s][k % 2][:].rearrange("p (e n) -> p e n", e=4), ps.rearrange("p (e n) -> p e n", e=4),
                        w[s][:, t, 4 * f:4 * f + 4].rearrange("p (e o) -> p e o", o=1).broadcast_to([P, 4, P]),
                        ALU.mult).then_inc(done, 1)
                elif name == "mx8":
                    if s == "F":
                        nc.vector.tensor_reduce(mx8[s][:, :, k], ps.rearrange("p (t n) -> p t n", t=QT), AX.X, ALU.max,
                                                negate=True).then_inc(done, 1)
                    else:
                        h, t = 2 * (k // 4) + k % 2, k // 2 % 2
                        nc.vector.tensor_reduce(mx8[s][:, t, h:h + 1], ps, AX.X, ALU.max, negate=True).then_inc(done, 1)
                elif name == "mT8":
                    link(nc.vector.tensor_copy(m2[s][:, 0, :], ps[0:H8, 0:SEQ]))
                    nc.vector.tensor_tensor(m2[s][:, 1, :], ps[0:H8, 0:SEQ], m2[s][:, 0, :], ALU.subtract)\
                        .then_inc(done, 1)

            link_of = {s: [0] for s in "XFKB"}
            run(dve, step)
            assert all(link_of[s][0] == COUNTS[s]["vch"] for s in "XFKB"), link_of

        @block.gpsimd
        def _(pool):
            for (s, n), credit in CREDIT.items():
                pool.sem_inc(S[s][n], credit)
            for tile in (ones, cT["X"], cT["K"], k8["F"], k8["B"], v8["F"], v8["B"]):
                pool.memset(tile[:], 1.0).then_inc(c_set, 1)
            pool.memset(nhalf[:], -0.5)
            pool.wait_ge(w_loaded, W_LOADS)
            pool.wait_ge(tanh_done, 1)
            for n, s in enumerate("XB"):
                pool.tensor_scalar(bo[s][:], bo[s][:], gates[:, n:n + 1], None, ALU.mult).then_inc(bias_done, 1)
            pool.wait_ge(bias_done, 2)

            def step(b, name, k, ring):
                s, m = b.s, S[b.s]
                calls = link_of[s]
                if k == 0 and name == "ln":
                    calls[0] = 0

                def link(ins):
                    calls[0] += 1
                    ins.then_inc(m["pch"], 1)
                    pool.wait_ge(m["pch"], b.value("pch", calls[0]))

                if name == "ln":
                    pool.wait_ge(m["mv"], b.value("mv", k + 1))
                    apart(pool)
                    link(pool.tensor_scalar(ve[s][:], mv[s][:, :, 1], EPS, None, ALU.add))
                    pool.tensor_tensor(rstd[s][:], ve[s][:], nhalf[:], ALU.pow).then_inc(m["rstd"], 1)
                    if s != "F" and k == 0:
                        pool.wait_ge(*b.before("sm"))
                        pool.tensor_tensor(xb[s][:], source[s, 0][:], bo[s][:].rearrange("p (o n) -> p o n", o=1)
                                           .broadcast_to([P, QT, P]), ALU.add).then_inc(m["xb"], 1)
                elif name == "e":
                    pool.wait_ge(*b.done("e", k))
                    if k >= 4:
                        pool.wait_ge(m["pv"], b.value("pv", (k - 4) // 2 + 1))
                    pool.wait_ge(m["psum"], b.value("psum", k))
                    p = prob[s][k % SLOTS[s]]
                    link(pool.tensor_tensor(half[:], p[:, 0:2 * SEQ], p[:, 2 * SEQ:], ALU.add))
                    pool.tensor_tensor(psum_k[k % 4][:], half[:, 0:SEQ], half[:, SEQ:], ALU.add).then_inc(m["psum"], 1)
                elif name == "moe":
                    t, f = divmod(k, 2)
                    pr_ = prod[s][k % 2]
                    pool.wait_ge(*b.done("moe", k))
                    link(pool.tensor_tensor(pr_[:, 0:2 * P], pr_[:, 0:2 * P], pr_[:, 2 * P:], ALU.add))
                    if f == 0:
                        pool.tensor_tensor(acc[s][:, t, :], pr_[:, 0:P], pr_[:, P:2 * P], ALU.add).then_inc(m["used"], 1)
                        return
                    link(pool.tensor_tensor(pr_[:, 0:P], pr_[:, 0:P], pr_[:, P:2 * P], ALU.add))
                    pool.tensor_tensor(acc[s][:, t, :], acc[s][:, t, :], pr_[:, 0:P], ALU.add).then_inc(m["used"], 1)
                    if k < 3:
                        return
                    pool.wait_ge(m["used"], b.value("used", 4))
                    pool.wait_ge(m["w"], b.value("w", 1))
                    apart(pool)
                    if s == "F":
                        link(pool.tensor_scalar(acc[s][:], acc[s][:], gates[:, 2:3], None, ALU.mult))
                        pool.wait_ge(*b.before("sm"))
                    else:
                        for t in range(QT):
                            last = pool.tensor_scalar(acc[s][:, t, :], acc[s][:, t, :], cb[:, t:t + 1], gates[:, 3:4],
                                                      ALU.add, ALU.mult)
                        link(last)
                        pool.wait_ge(m["out"], b.value("out", 0))
                    pool.tensor_tensor(fin[s][:], acc[s][:], x1[s][:], ALU.add).then_inc(m["fin"], 1)
            link_of = {s: [0] for s in "XFKB"}
            run(pool, step)
            assert all(link_of[s][0] == COUNTS[s]["pch"] for s in "XFB"), link_of


def kernel(**inputs):
    import concourse.bacc as bacc
    from concourse.bass_utils import run_bass_kernel_spmd

    g = {k: np.asarray(v) for k, v in inputs.items()}

    def dh(m):
        return m.reshape(m.shape[:-1] + (H8, D8)).swapaxes(-1, -2).reshape(m.shape)

    wqkv, bqkv = g["L0_ffn_W_qkv"], g["L0_ffn_b_qkv"]
    wkv, bkv = g["L1_xattn_Wkv"], g["L1_xattn_bkv"]
    arrays = {
        "x": g["x"], "ctxT": g["ctx_768"].transpose(0, 2, 1), "g_xattn": g["g_xattn"], "g_ffn": g["g_ffn"],
        "ident": np.eye(P, dtype=np.float32),
        "iota": np.tile(np.arange(NE, dtype=np.float32), (P, 1)),
        "wqT": g["L0_xattn_Wq"].reshape(P, XH, XD).transpose(2, 1, 0),
        "wkT": g["L0_xattn_Wk"].reshape(CD, XH, XD).transpose(2, 1, 0),
        "wvx": g["L0_xattn_Wv"], "wox": g["L0_xattn_Wo"].reshape(XH // 2, P, P).transpose(1, 0, 2),
        "boX": g["L0_xattn_bo"], "boB": g["L1_xattn_bo"],
        "wq8F": dh(wqkv[:, :P]), "wk8F": dh(wqkv[:, P:2 * P]), "wv8F": wqkv[:, 2 * P:],
        "bq8F": dh(bqkv[:2 * P].reshape(2, P)).T, "bv8F": bqkv[2 * P:],
        "wq8B": dh(g["L1_xattn_Wq"]), "wk8B": dh(wkv[:, :P]), "wv8B": wkv[:, P:],
        "bq8B": np.stack([dh(g["L1_xattn_bq"]), dh(bkv[:P])], axis=1), "bv8B": bkv[P:],
        "wo8": g["L1_xattn_Wo"],
        "wgF": g["L0_ffn_W_gate"], "wgB": g["L1_ffn_router_w"].T, "bg": g["L0_ffn_b_gate"],
        "weF": g["L0_ffn_W_experts"], "weB": g["L1_ffn_expert_weights"], "be": g["L0_ffn_b_experts"],
    }
    arrays = {"in_" + k: np.ascontiguousarray(v) for k, v in arrays.items()}
    nc = bacc.Bacc("TRN2", target_bir_lowering=False, num_devices=1)
    handles = {k[3:]: nc.dram_tensor(k, v.shape, mybir.dt.from_np(v.dtype), kind="ExternalInput").ap()
               for k, v in arrays.items()}
    out = nc.dram_tensor("out", (BATCH, SEQ, P), F32, kind="ExternalOutput").ap()
    build(nc, handles, out)
    r = run_bass_kernel_spmd(nc, [arrays], core_ids=[0])
    return r.results[0]["out"]
```

```python
from contextlib import ExitStack

import numpy as np
import concourse.bass as bass
from concourse import mybir

ALU = mybir.AluOpType
ACT = mybir.ActivationFunctionType
AX = mybir.AxisListType
F32 = mybir.dt.float32
BF16 = mybir.dt.bfloat16
U32 = mybir.dt.uint32

P = 128
BATCH, SEQ, KV, CD = 8, 256, 512, 96
QT = SEQ // P
XH, XD = 8, 64
H8, D8 = 16, 8
NPAIR = H8 // 2
NE = 8
KROWS = 6 * D8
MROWS = KROWS + 2
EPS = 1e-5
QPART = (0, 1, 2, 0, 1, 0)
KPART = (0, 0, 0, 1, 1, 2)

KEYS = {"F": SEQ, "B": KV}
SLOTS = {"X": 4, "F": 4, "B": 8}
WIDE = {"F": 2 * SEQ, "B": SEQ, "K": KV}


BETWEEN = {'vp': (17, 17), 'moe': (0, 0, 0, 3)}


def stage_steps(s):
    def norm(k):
        return [("ls", k, 0, "", 0, 0, 1.1), ("ln", k, .4, "sm", .4, .2, .7)]

    def spread(steps, others, places):
        new = []
        for n, step in enumerate(steps + [None]):
            new += [other for other, place in zip(others, places) if place == n] + [step] * (step is not None)
        return new

    t = []
    if s == "X":
        t += norm(0) + [("qp", 0, 1.7, "st", 2.2, .2, 0), ("qp", 1, 1.7, "st", 2.2, 0, 0)]
        maxima = [("mx", k, .22, "sm", .62, .3 if k == 0 else 0, 0) for k in range(XH * QT)] + [("mT", 0, .4, "sm", .4, .3, 0)]
        t += spread(maxima, [("vp", k, 1.7, "st", 1.1, 0, 0) for k in range(2)], BETWEEN["vp"])
    if s == "x":
        for u in range(XH):
            t.append(("e", u, 1.75, "st", 1.1, 4. if u == 0 else 0, 0))
            if u % 2 == 0 and u > 0:
                t.append(("pv", u // 2 - 1, 2.3, "", 0, 0, 0))
            if u % 2 == 1 and u > 1:
                t.append(("nx", u // 2 - 1, 0, "", 0, 0, 2.2))
        t += [("pv", XH // 2 - 1, 2.3, "", 0, 2.5, 0), ("nx", XH // 2 - 1, 0, "", 0, 0, 2.2), ("out", 0, 1.8, "sm", .5, .1, 0)]
    if s == "F":
        t += norm(0) + [("qk", 0, .9, "st", 1.6, .2, 0), ("gate", 0, .1, "sm", .5, 0, 0), ("sp", 0, 0, "", 0, .3, 2.2)]
        t += [("v8", 0, .5, "sm", .5, 0, 0), ("gx", 0, 0, "", 0, .5, 2.8)]
        t += spread([("mx8", k, .22, "sm", .62, 1. if k == 0 else 0, 0) for k in range(H8)],
                    [("moe", k, .85, "sm", .65, .1, 0) for k in range(4)], BETWEEN["moe"])
        t += [("mT8", 0, .4, "sm", .6, .3, 0), ("wT", 0, .4, "sm", .3, 0, 0), ("wb", 0, .4, "sm", .3, .3, 0)]
    if s == "f":
        for u in range(NPAIR):
            t.append(("e8", u, .45, "st", 1.1, 4. if u == 0 else 0, 0))
            if u % 2 == 0 and u > 0:
                t.append(("pv8", u // 2 - 1, .7, "pn", 0, 0, 0))
            if u % 2 == 1 and u > 1:
                t.append(("ev8", u // 2 - 1, 0, "", 0, 0, .3))
        t += [("pv8", 3, .7, "pn", 0, 1.2, 0), ("ev8", 3, 0, "", 0, .1, .3), ("oT", 0, .8, "sm", .7, .1, 0), ("oT", 1, .8, "sm", .7, 0, 0)]
    if s == "K":
        t += [("cx", 0, 0, "", 0, 0, 0), ("kk", 0, .9, "st", 1.2, 4., 0), ("sp", 0, 0, "", 0, 0, 1.8)]
        t += [("vv", 0, .5, "sm", .5, 0, 0), ("vv", 1, .5, "sm", .5, 0, 0)]
    if s == "B":
        t += norm(0) + [("qk", 0, .45, "sm", .8, .2, 0), ("sp", 0, 0, "", 0, 0, 1.2)]
    if s == "b":
        t += [("mx8", k, .22, "sm", .62, 0, 0) for k in range(H8 * QT)]
        t += [("mT8", 0, .4, "sm", .6, .3, 0)]
        for u in range(2 * NPAIR):
            t.append(("e8", u, .45, "st", 1.1, 5. if u == 0 else 0, 0))
            if u % 4 == 0 and u > 0:
                t.append(("pv8", u // 4 - 1, 1.6, "pn", 0, 0, 0))
            if u % 4 == 2 and u > 4:
                t.append(("ev8", u // 4 - 1, 0, "", 0, 0, .3))
        t += [("pv8", 3, 1.6, "pn", 0, 1.2, 0), ("ev8", 3, 0, "", 0, .1, .3), ("oT", 0, .8, "sm", .6, .1, 0), ("oT", 1, .8, "sm", .6, 0, 0)]
        t += [("aT", 0, .4, "sm", .4, .2, 0), ("out8", 0, .5, "sm", .5, .2, 0)]
    if s == "c":
        t += norm(0) + [("gate", 0, .1, "sm", .6, .2, 0), ("gx", 0, 0, "", 0, .3, 3.6)]
        t += [("moe", k, .85, "sm", .65, .1, 0) for k in range(4)]
    return t


AFTER = {("F", "ls"): ("x", "out", 0),
         ("B", "ls"): ("f", "oT", 1),
         ("b", "aT"): ("c", "moe", 3),
         ("K", "kk"): ("b", "pv8", 3)}

LINES = {"X": "xX", "F": "fF", "K": "K", "B": "bB", "C": "c"}
LAG = dict(x=0, X=-1, f=1, F=0, K=1, B=1, b=2, c=3)
ROUNDS = [[s for s in LAG if 0 <= r - LAG[s] < BATCH] for r in range(-1, BATCH + 3)]
FULL = [r for r, stages in enumerate(ROUNDS, -1) if len(stages) == len(LAG)]


STEER = {
    -1: (0.105, 3.5, {'F': 5, 'B': 8, 'C': 5}, {'F': 0.5, 'K': 0.5, 'C': -1.5}),
    0: (0.1, 3, {'F': 5, 'C': 5}, {'F': 0.5, 'K': 0.5, 'C': -1}),
    1: (0.3, 2.5, {'F': 5, 'C': 5}, {'F': 0.5, 'K': 0.5, 'B': -2, 'C': -1}),
    2: (0.059, 1.0, {'F': 5, 'C': 5}, {'F': 0.5, 'K': -0.5, 'C': -1}),
    3: (0.05, 1.5, {'F': 5, 'B': 2, 'C': 5}, {'F': 0.5, 'K': 0.5, 'C': -0.5}),
    7: (0.1, 2.5, {'F': 5, 'C': 5}, {'X': -4, 'F': 0.5, 'K': 2.5, 'C': -1}),
    8: (0.06, 4.5, {'F': 5, 'C': 5}, {'X': 4, 'F': 0.5, 'K': 4.5, 'C': -1}),
    9: (0.15, 3, {'F': 5, 'B': 2, 'C': 5}, {'F': 4.5, 'K': 0.5, 'B': -0.5, 'C': -1}),
    10: (0.1, 3, {'F': 5, 'C': 5}, {'F': 0.5, 'K': 0.5, 'C': -1}),
}
GPSIMD = {"ls": 1., "e": 1.9, "moe": 1.8}


def merge(stages, steer):
    lines = {n: [(s, *step) for s in line if s in stages for step in stage_steps(s)] for n, line in LINES.items()}
    urgent, lead, hold, handicap = steer
    ready = {n: hold.get(n, 0.) for n in lines}
    free = {"st": [0., 0.], "sm": [0., 0.], "pn": [0., 0.]}
    dve = act = pe = pool = 0.
    order, seen, held = [], set(), False
    while any(lines.values()):
        best = None
        for n, line in lines.items():
            if not line:
                continue
            s, name, k, cost, ring, took, gap, own = line[0]
            other = AFTER.get((s, name))
            if other and other[0] in stages and other not in seen:
                continue
            if name == "pv8" and held:
                continue
            start = ready[n] + gap
            if name == "ev8":
                start = max(start, act)
            elif own:
                start = max(start, dve)
            if name == "pv":
                start = max(start, pool - 1.5)
            if cost:
                start = max(start + own, pe, free[ring][-2] if ring else 0.)
            key = start + handicap.get(n, 0.) - (lead if own else 0.) - urgent * sum(x[3] + x[5] + x[6] + x[7] for x in line)
            if best is None or key < best[0]:
                best = (key, start, n)
        _, start, n = best
        s, name, k, cost, ring, took, gap, own = lines[n].pop(0)
        seen.add((s, name, k))
        held = name == "pv8" or held and name != "ev8"
        if cost:
            if own:
                dve = max(start, dve)
            end = pe = start + cost
            if ring in ("st", "sm"):
                end = max(dve if ring == "sm" else act, end) + took
                free[ring].append(end)
                if ring == "sm":
                    dve = end
                else:
                    act = end
            if name in GPSIMD:
                pool = max(pool, end) + GPSIMD[name]
            nxt = lines[n][0] if lines[n] else None
            if nxt and nxt[6] == 0 and not nxt[7]:
                end = pe
        else:
            end = start + own
            if name == "ev8":
                act = end
            elif own:
                dve = end
            if name == "ls":
                end = max(pool, end) + GPSIMD[name]
                pool = end + (1. if s in "XB" else 0.)
        ready[n] = end
        order.append((s, name, k, ring))
    return order


ORDER = [merge(stages, STEER[FULL[0] if r in FULL else r]) for r, stages in enumerate(ROUNDS, -1)]
FILLS = [{r: sum(step[3] == r for step in order) for r in ("st", "sm", "pn")} for order in ORDER]

COUNTS = {
    "X": dict(xin=16, ctx=16, mv=1, rstd=1, xh=1, xb=1, ctb=1, mroww=16, mrowr=16, psum=XH, pv=XH // 2, norm=XH // 2,
              pch=9, vch=5),
    "F": dict(mv=1, rstd=1, xh=1, split=1, splitw=16, qks=18 * 16, lg=1, eg=1, w=1, used=4, fin=1, m2w=16, m2r=32,
              xm=2, pch=8, vch=14),
    "K": dict(ctx=16, split=1, splitw=16, qks=12 * 16, vch=2),
    "B": dict(mv=1, rstd=1, xh=1, xb=1, split=1, splitw=16, qks=6 * 16, m2w=16, m2r=32, pch=1, vch=6),
    "C": dict(mv=1, rstd=1, xh=1, lg=1, eg=1, w=1, used=4, fin=1, out=16, pch=8, vch=15),
}
FIRST = {s: stage_steps(s)[0][:2] for s in LAG}
LINKS_BEFORE = {"dve": {"x": 1, "f": 12, "b": 3}, "pool": {"x": 1, "b": 1}}

CREDIT = {("C", "used"): 2, ("F", "used"): 2, ("C", "out"): 16}


def build(nc, a, out):
    ctx = ExitStack()
    with ctx:
        def sb(name, shape, dt=F32):
            return ctx.enter_context(nc.sbuf_tensor(name, shape, dt))

        def dram(name, shape, dt):
            return nc.dram_tensor(name, shape, dt, kind="Internal").ap()

        def sem(name):
            return ctx.enter_context(nc.semaphore(name))

        ident = sb("ident", [P, P])
        iota = sb("iota", [P, NE])
        ones = sb("ones", [P, XD])
        wqk = sb("wqk", [P, XH, CD])
        wvx = sb("wvx", [CD, XH * XD])
        wox = sb("wox", [P, XH // 2, P])
        gates = sb("gates", [P, 4])
        graw = sb("graw", [P, 4])
        bo = {s: sb("bo" + s, [P, P]) for s in "XB"}
        wq8 = {s: sb("wq8" + s, [P, P]) for s in "FB"}
        wk8 = {"F": sb("wk8F", [P, P]), "B": sb("wk8B", [CD, P])}
        wv8 = {"F": sb("wv8F", [P, P]), "B": sb("wv8B", [CD, P])}
        bq8 = {s: sb("bq8" + s, [P, 2]) for s in "FB"}
        bv8 = {s: sb("bv8" + s, [P, P]) for s in "FB"}
        wo8 = sb("wo8", [P, P])
        wg = {s: sb("wg" + s, [P, NE]) for s in "FB"}
        bg = sb("bg", [P, NE])
        we = {s: sb("we" + s, [P, NE * P]) for s in "FB"}
        be = sb("be", [NE, P])
        nhalf = sb("nhalf", [P, QT])

        def per(streams, name, shape, dt=F32):
            return {s: sb(name + s, shape, dt) for s in streams}

        xin = sb("xin", [P, QT, P])
        x1 = {"F": sb("x1", [P, QT, P]), "B": sb("x3", [P, QT, P])}
        xmid = sb("xmid", [P, QT, P])
        source = {("X", 0): xin, ("F", 0): x1["F"], ("B", 0): xmid, ("C", 0): x1["B"]}
        cT = per("XK", "cT", [CD + 1, KV])
        xb = per("XB", "xb", [P, QT, P])
        st6 = per("XFB", "st6", [P, QT, 6])
        mv = per("XFB", "mv", [P, QT, 2])
        ve = per("XFB", "ve", [P, QT])
        rstd = per("XFB", "rstd", [P, QT])
        xh = per("XFB", "xh", [P, QT, P])
        xT = per("XFB", "xT", [P, SEQ])
        qA = sb("qA", [CD + 1, XH, SEQ])
        qAb = sb("qAb", [CD, XH, SEQ], BF16)
        cTb = sb("cTb", [CD, KV], BF16)
        vX = sb("vX", [P, KV // P, XH * XD])
        mxA = sb("mxA", [P, QT, XH])
        mrow = sb("mrow", [XH, SEQ])
        prob = {s: [sb(f"prob{s}{n}", [P, 4 * SEQ]) for n in range(SLOTS[s])] for s in "XFB"}
        wqT = prob["X"][0][0:XD, 0:XH * P].rearrange("p (h n) -> p h n", h=XH)
        wkT = prob["X"][1][0:XD, 0:XH * CD].rearrange("p (h n) -> p h n", h=XH)
        half = sb("half", [P, 2 * SEQ])
        psum_k = [sb(f"psum_k{n}", [P, SEQ]) for n in range(4)]
        rden = sb("rden", [P, SEQ])
        oTX = sb("oTX", [P, XH // 2, SEQ])
        qk = {s: sb("qk" + s, [P, WIDE[s]]) for s in "FKB"}
        parts = {s: sb("parts" + s, [P, 3, WIDE[s]], BF16) for s in "FKB"}
        q8 = {s: sb("q8" + s, [P, NPAIR, SEQ], BF16) for s in "FB"}
        k8 = {s: sb("k8" + s, [P, NPAIR, KEYS[s]], BF16) for s in "FB"}
        v8 = {s: sb("v8" + s, [P, KEYS[s] // P, H8, 32]) for s in "FB"}
        mx8 = per("FB", "mx8", [P, QT, H8])
        m2 = per("FB", "m2", [H8, 2, SEQ], BF16)
        oU = per("FB", "oU", [P, 4, SEQ])
        rr = per("FB", "rr", [P, QT, H8])
        att = per("FB", "att", [P, QT, P])
        attT = xT["B"]
        lg = per("FB", "lg", [P, QT, NE])
        nm = per("FB", "nm", [P, QT])
        eg = per("FB", "eg", [P, QT, NE])
        sg = per("FB", "sg", [P, QT])
        pr = per("FB", "pr", [P, QT, NE])
        top = per("FB", "top", [P, QT, 8])
        tix = per("FB", "tix", [P, QT, 8], U32)
        tif = per("FB", "tif", [P, QT, 8])
        w0 = per("FB", "w0", [P, QT, NE])
        w1 = per("FB", "w1", [P, QT, NE])
        w = per("FB", "w", [P, QT, NE])
        ts = sb("ts", [P, QT])
        wp = sb("wp", [P, QT, NE])
        cb = sb("cb", [P, QT])
        wT = sb("wT", [NE, SEQ])
        prod = {s: [sb(f"prod{s}{n}", [P, 4 * P]) for n in range(2)] for s in "FB"}
        acc = per("FB", "acc", [P, QT, P])
        fin = per("FB", "fin", [P, QT, P])

        for d in (wg, we, x1, st6, mv, ve, rstd, xh, xT, lg, nm, eg, sg, pr, top, tix, tif, w0, w1, w, prod, acc, fin):
            d["C"] = d["B"]

        mrow_d = dram("mrow_d", [XH, SEQ], F32)
        part_d = {s: dram("part_d" + s, [3, P, WIDE[s]], BF16) for s in "FKB"}
        m2_d = {s: dram("m2_d" + s, [2, H8, SEQ], BF16) for s in "FB"}

        st = ctx.enter_context(nc.psum_tensor("st", [P, 2, 1024], F32))
        sm = ctx.enter_context(nc.psum_tensor("sm", [P, 2, 512], F32))
        pvx = ctx.enter_context(nc.psum_tensor("pvx", [P, 512], F32))
        pv8 = ctx.enter_context(nc.psum_tensor("pv8", [P, 512], F32))

        ring_full = {r: sem(r + "_full") for r in ("st", "sm", "pn")}
        ring_done = {r: sem(r + "_done") for r in ("st", "sm", "pn")}
        ring_psum = {"st": st, "sm": sm}
        S = {s: {n: sem(n + s) for n in COUNTS[s]} for s in COUNTS}
        w_first, w_loaded, c_set, tanh_done, bias_done = sem("w_first"), sem("w_loaded"), sem("c_set"), sem("tanh_done"), sem("bias_done")
        passed = sem("passed")
        fold_ps, fold_ev = sem("fold_ps"), sem("fold_ev")

        class Stream:

            def __init__(self, stage, batch, base, places):
                self.stage, self.s = stage, stage.upper()
                self.batch, self.base, self.places = batch, base, places

            def value(self, n, k):
                return self.batch * COUNTS[self.s][n] + (k + CREDIT.get((self.s, n), 0))

            def place(self, name, k):
                ring, n = self.places[self.stage, name, k]
                reg, const = self.base[ring]
                return ring, reg, const + n

            def slot(self, name, k):
                ring, _, n = self.place(name, k)
                return ring_psum[ring][:, n % 2, :] if ring != "pn" else pv8[:]

            def full(self, name, k):
                ring, reg, n = self.place(name, k)
                return ring_full[ring], reg + (n + 1)

            def done(self, name, k=0):
                ring, reg, n = self.place(name, k)
                return ring_done[ring], reg + (n + 1)

            def beside(self, stage):
                return Stream(stage, 0, self.base, self.places)

            def before(self, ring):
                reg, const = self.base[ring]
                return ring_done[ring], reg + const

        def run(eng, step):
            def one_round(stages, order, number, base):
                places, n = {}, {r: 0 for r in base}
                for s, name, k, ring in order:
                    if ring:
                        places[s, name, k] = (ring, n[ring])
                        n[ring] += 1
                at = {s: Stream(s, number - LAG[s], base, places) for s in stages}
                for s, name, k, ring in order:
                    step(at[s], name, k, ring)

            before = {r: 0 for r in ("st", "sm", "pn")}
            for i, (stages, order, fills) in enumerate(zip(ROUNDS, ORDER, FILLS)):
                if i == 1:
                    eng.wait_ge(w_loaded, W_LOADS)
                    eng.wait_ge(c_set, MEMSETS)
                if i - 1 not in FULL:
                    one_round(stages, order, i - 1, {r: (0, before[r]) for r in before})
                elif i - 1 == FULL[0]:
                    assert fills["st"] % 2 == 0 and fills["sm"] % 2 == 0
                    with eng.Fori(0, len(FULL)) as j:
                        one_round(stages, order, j + FULL[0], {r: (j * fills[r], before[r]) for r in before})
                before = {r: before[r] + fills[r] for r in before}

        NC = {s: KEYS[s] // P for s in "FB"}
        block = ctx.enter_context(nc.Block())

        def apart(eng):
            eng.sem_inc(passed, 1)

        loads = [(wo8[:], a["wo8"]), (iota[:], a["iota"]), (wox[:], a["wox"]),
                 (be[:], a["be"]), (bg[:], a["bg"].rearrange("(o n) -> o n", o=1).broadcast_to([P, NE]))]
        for s in "FB":
            loads += [(wq8[s][:], a["wq8" + s]), (wk8[s][:], a["wk8" + s]), (wv8[s][:], a["wv8" + s]),
                      (bq8[s][:], a["bq8" + s]),
                      (bv8[s][:], a["bv8" + s].rearrange("(o n) -> o n", o=1).broadcast_to([P, P])),
                      (wg[s][:], a["wg" + s]),
                      (we[s][:].rearrange("p (e n) -> p e n", e=NE), a["we" + s].rearrange("e k n -> k e n"))]
        first = [(ident[:], a["ident"]), (wqT, a["wqT"]), (wkT, a["wkT"]),
                 (graw[:, 0:2], a["g_xattn"].rearrange("(o n) -> o n", o=1).broadcast_to([P, 2])),
                 (graw[:, 2:4], a["g_ffn"].rearrange("(o n) -> o n", o=1).broadcast_to([P, 2]))]
        first += [(bo[s][:], a["bo" + s].rearrange("(o n) -> o n", o=1).broadcast_to([P, P])) for s in "XB"]
        first += [(wvx[:], a["wvx"])]
        W_FIRST, W_LOADS = 16 * len(first), 16 * len(loads)
        MEMSETS = 7

        @block.sync
        def _(sp):
            def load_x(batch):
                sp.dma_start(xin[:], a["x"][bass.ds(batch, 1)].rearrange("o (t p) n -> p (o t) n", p=P))\
                    .then_inc(S["X"]["xin"], 16)

            def load_ctx(s, batch):
                sp.dma_start(cT[s][0:CD], a["ctxT"][bass.ds(batch, 1)].rearrange("o c t -> (o c) t"))\
                    .then_inc(S[s]["ctx"], 16)

            load_x(0)
            for dst, src in first:
                sp.dma_start(dst, src).then_inc(w_first, 16)
            sp.wait_ge(c_set, 1)
            load_ctx("X", 0)
            for dst, src in loads:
                sp.dma_start(dst, src).then_inc(w_loaded, 16)
            sp.wait_ge(c_set, MEMSETS)

            def step(b, name, k, ring):
                s, m = b.s, S[b.s]
                if (s, name) == ("X", "mT"):
                    sp.wait_ge(*b.done("mT"))
                    sp.dma_start(mrow_d, mrow[:]).then_inc(m["mroww"], 16)
                    sp.wait_ge(m["mroww"], b.value("mroww", 16))
                    sp.dma_start(qA[CD:CD + 1], mrow_d.rearrange("(o h) n -> o h n", o=1)).then_inc(m["mrowr"], 16)
                if (s, name, k) == ("X", "e", 0):
                    sp.wait_ge(m["xb"], b.value("xb", 1))
                    load_x((b.batch + 1) % BATCH)
                if (s, name, k) == ("X", "e", XH - 1):
                    sp.wait_ge(*b.done("e", XH - 1))
                    load_ctx("X", (b.batch + 1) % BATCH)
                if name == "cx":
                    sp.wait_ge(*b.before("sm"))
                    sp.wait_ge(*b.before("st"))
                    load_ctx("K", b.batch)
                if name == "sp":
                    sp.wait_ge(m["split"], b.value("split", 1))
                    sp.dma_start(part_d[s].rearrange("t p n -> p t n"), parts[s][:]).then_inc(m["splitw"], 16)
                    sp.wait_ge(m["splitw"], b.value("splitw", 16))
                    src = part_d[s].rearrange("t (d p i) n -> i (t d) p n", i=2, p=NPAIR)
                    for i in range(2):
                        if s != "K":
                            for j0, n in ((0, 3), (3, 2), (5, 1)):
                                r = 64 * i + D8 * j0
                                sp.dma_start(q8[s][r:r + D8 * n], src[i, 0:D8 * n, :, 0:SEQ]).then_inc(m["qks"], 16)
                        if s != "B":
                            for j in range(6):
                                r, t = 64 * i + D8 * j, D8 * KPART[j]
                                keys = k8["F" if s == "F" else "B"]
                                sp.dma_start(keys[r:r + D8], src[i, t:t + D8, :, SEQ * (s == "F"):])\
                                    .then_inc(m["qks"], 16)
                if name == "mT8":
                    sp.wait_ge(*b.done("mT8"))
                    sp.dma_start(m2_d[s].rearrange("t h n -> h t n"), m2[s][:]).then_inc(m["m2w"], 16)
                    sp.wait_ge(m["m2w"], b.value("m2w", 16))
                    for i in range(2):
                        sp.dma_start(q8[s][64 * i + KROWS:64 * i + MROWS],
                                     m2_d[s].rearrange("t (p i) n -> i t p n", i=2)[i]).then_inc(m["m2r"], 16)
                if (s, name, k) == ("C", "moe", 3):
                    sp.wait_ge(m["fin"], b.value("fin", 1))
                    sp.dma_start(out[bass.ds(b.batch, 1)].rearrange("o (t p) n -> p (o t) n", p=P), fin["B"][:])\
                        .then_inc(m["out"], 16)
            run(sp, step)
            sp.wait_ge(S["C"]["out"], 16 * BATCH + CREDIT["C", "out"])
            sp.wait_ge(S["X"]["xin"], 16 * (BATCH + 1))

        @block.tensor
        def _(pe):
            pe.wait_ge(w_first, W_FIRST)
            for h in range(XH):
                fold = nc.tensor.matmul(st[:, h // 4, (h % 4) * P:(h % 4) * P + CD], wqT[:, h, :], wkT[:, h, :],
                                        start=True, stop=True)
            fold.then_inc(fold_ps, 1)
            pe.wait_ge(fold_ev, 2)

            def step(b, name, k, ring):
                s, m = b.s, S[b.s]
                if ring:
                    _, reg, n = b.place(name, k)
                    depth = 1 if ring == "pn" else 2
                    if not isinstance(reg, int) or n >= depth:
                        pe.wait_ge(ring_done[ring], reg + (n + 1 - depth))
                    ps = b.slot(name, k)
                mm, last = nc.tensor.matmul, None
                if name == "ln":
                    pe.wait_ge(m["xh"], b.value("xh", k + 1))
                    for t in range(QT):
                        last = nc.tensor.transpose(ps[:, t * P:(t + 1) * P], xh[s][:, t, :], ident[:])
                elif name == "qp":
                    pe.wait_ge(*b.done("ln"))
                    for j in range(4):
                        last = mm(ps[0:CD, j * SEQ:(j + 1) * SEQ], wqk[:, 4 * k + j, :], xT[s][:], start=True, stop=True)
                elif name == "vp":
                    pe.wait_ge(m["ctx"], b.value("ctx", 16))
                    for j in range(2):
                        c = 2 * k + j
                        last = mm(ps[:, j * 512:(j + 1) * 512], cT["X"][0:CD, c * P:(c + 1) * P], wvx[:],
                                  start=True, stop=True)
                elif name == "mx":
                    h, t = divmod(k, QT)
                    pe.wait_ge(*b.done("qp", h // 4))
                    pe.wait_ge(m["ctb"], b.value("ctb", 1))
                    last = mm(ps, qAb[:, h, t * P:(t + 1) * P], cTb[:], start=True, stop=True)
                elif name == "mT":
                    pe.wait_ge(*b.done("mx", XH * QT - 1))
                    for t in range(QT):
                        last = nc.tensor.transpose(ps[0:XH, t * P:(t + 1) * P], mxA[:, t, :], ident[:])
                elif name == "e":
                    pe.wait_ge(m["mrowr"], b.value("mrowr", 16))
                    for c in range(KV // P):
                        last = mm(ps[:, c * SEQ:(c + 1) * SEQ], cT["X"][:, c * P:(c + 1) * P], qA[:, k, :],
                                  start=True, stop=True)
                elif name == "pv":
                    pe.wait_ge(*b.done("e", 2 * k + 1))
                    if k > 0:
                        pe.wait_ge(m["norm"], b.value("norm", k))
                    pe.wait_ge(*b.before("st"))
                    for c in range(KV // P):
                        for i in range(2):
                            h = 2 * k + i
                            mm(pvx[64 * i:64 * i + 64, 0:SEQ], vX[:, c, h * XD:(h + 1) * XD],
                               prob[s][h % SLOTS[s]][:, c * SEQ:(c + 1) * SEQ], start=(c == 0), stop=(c == KV // P - 1))
                    pe.wait_ge(m["psum"], b.value("psum", 2 * k + 2))
                    for i in range(2):
                        ins = mm(pvx[64 * i:64 * i + 64, SEQ:2 * SEQ], ones[:], psum_k[(2 * k + i) % 4][:],
                                 start=True, stop=True)
                    ins.then_inc(m["pv"], 1)
                elif name == "out":
                    pe.wait_ge(m["norm"], b.value("norm", XH // 2))
                    for t in range(QT):
                        for j in range(XH // 2):
                            last = mm(ps[:, t * P:(t + 1) * P], oTX[:, j, t * P:(t + 1) * P], wox[:, j, :],
                                      start=(j == 0), stop=(j == XH // 2 - 1))
                elif name == "qk":
                    pe.wait_ge(*b.done("ln"))
                    last = mm(ps[:, 0:SEQ], wq8[s][:], xT[s][:], start=True, stop=True)
                    if s == "F":
                        last = mm(ps[:, 512:512 + SEQ], wk8[s][:], xT[s][:], start=True, stop=True)
                elif name == "kk":
                    pe.wait_ge(m["ctx"], b.value("ctx", 16))
                    last = mm(ps[:, 0:KV], wk8["B"][:], cT["K"][0:CD, :], start=True, stop=True)
                elif name in ("v8", "vv"):
                    if s == "F":
                        pe.wait_ge(*b.done("ln"))
                    for j in range(2):
                        c = 2 * k + j
                        tok = xT["F"][:, c * P:(c + 1) * P] if s == "F" else cT["K"][0:CD, c * P:(c + 1) * P]
                        last = mm(ps[:, j * P:(j + 1) * P], tok, wv8["F" if s == "F" else "B"][:], start=True, stop=True)
                elif name == "gate":
                    pe.wait_ge(*b.done("ln"))
                    for t in range(QT):
                        last = mm(ps[:, t * NE:(t + 1) * NE], xT[s][:, t * P:(t + 1) * P], wg[s][:], start=True, stop=True)
                elif name == "moe":
                    t, f = divmod(k, 2)
                    last = mm(ps, xT[s][:, t * P:(t + 1) * P], we[s][:, f * 512:(f + 1) * 512], start=True, stop=True)
                elif name == "mx8":
                    pe.wait_ge(m["qks"], b.value("qks", COUNTS[s]["qks"]))
                    if s == "F":
                        p, i = divmod(k, 2)
                        for t in range(QT):
                            last = mm(ps[:, t * SEQ:(t + 1) * SEQ], q8[s][64 * i:64 * i + KROWS, p, t * P:(t + 1) * P],
                                      k8[s][64 * i:64 * i + KROWS, p, :], start=True, stop=True)
                    else:
                        if k == 0:
                            pe.wait_ge(S["K"]["qks"], (b.batch + 1) * COUNTS["K"]["qks"])
                        p, t, i = k // 4, k // 2 % 2, k % 2
                        last = mm(ps, q8[s][64 * i:64 * i + KROWS, p, t * P:(t + 1) * P],
                                  k8[s][64 * i:64 * i + KROWS, p, :], start=True, stop=True)
                elif name == "mT8":
                    pe.wait_ge(*b.done("mx8", H8 * NC[s] // 2 - 1))
                    for t in range(QT):
                        last = nc.tensor.transpose(ps[0:H8, t * P:(t + 1) * P], mx8[s][:, t, :], ident[:])
                elif name == "wT":
                    pe.wait_ge(m["w"], b.value("w", 1))
                    for t in range(QT):
                        last = nc.tensor.transpose(ps[0:NE, t * P:(t + 1) * P], w[s][:, t, :], ident[:])
                elif name == "wb":
                    pe.wait_ge(*b.done("wT"))
                    for t in range(QT):
                        last = mm(ps[:, t * P:(t + 1) * P], wT[:, t * P:(t + 1) * P], be[:], start=True, stop=True)
                elif name == "e8":
                    pe.wait_ge(m["m2r"], b.value("m2r", 32))
                    p, c0 = (k, 0) if s == "F" else (k // 2, 2 * (k % 2))
                    for c in range(2):
                        for i in range(2):
                            last = mm(ps[:, 512 * i + SEQ * c:512 * i + SEQ * (c + 1)],
                                      k8[s][64 * i:64 * i + MROWS, p, (c0 + c) * P:(c0 + c + 1) * P],
                                      q8[s][64 * i:64 * i + MROWS, p, :], start=True, stop=True)
                elif name == "pv8":
                    n = NC[s]
                    pe.wait_ge(*b.done("e8", n * (k + 1) - 1))
                    pe.wait_ge(*b.before("sm"))
                    for c in range(n):
                        for i in range(4):
                            h = 4 * k + i
                            u = (h // 2) * (n // 2) + c // 2
                            o = 512 * (h % 2) + SEQ * (c % 2)
                            last = mm(ps[32 * i:32 * i + 32, 0:SEQ], v8[s][:, c, h, :], prob[s][u % SLOTS[s]][:, o:o + SEQ],
                                     start=(c == 0), stop=(c == n - 1), tile_position=(0, 32 * i))
                elif name == "oT":
                    pe.wait_ge(*b.done("pv8", 3))
                    for g in range(4):
                        last = nc.tensor.transpose(ps[:, g * P:(g + 1) * P], oU[s][:, g, k * P:(k + 1) * P], ident[:])
                elif name == "aT":
                    pe.wait_ge(*b.done("oT", 1))
                    for t in range(QT):
                        last = nc.tensor.transpose(ps[:, t * P:(t + 1) * P], att[s][:, t, :], ident[:])
                elif name == "out8":
                    pe.wait_ge(*b.done("aT"))
                    for t in range(QT):
                        last = mm(ps[:, t * P:(t + 1) * P], attT[:, t * P:(t + 1) * P], wo8[:], start=True, stop=True)
                if ring:
                    last.then_inc(ring_full[ring], 1)
            run(pe, step)

        @block.scalar
        def _(act):
            act.wait_ge(w_first, W_FIRST)
            nc.scalar.activation(gates[:], graw[:], ACT.Tanh).then_inc(tanh_done, 1)
            act.wait_ge(fold_ps, 1)
            for j in range(2):
                nc.scalar.activation(wqk[:, 4 * j:4 * j + 4, :],
                                     st[:, j, 0:4 * P].rearrange("p (h n) -> p h n", h=4)[:, :, 0:CD],
                                     ACT.Copy).then_inc(fold_ev, 1)

            def step(b, name, k, ring):
                s, m = b.s, S[b.s]
                if name == "gx":
                    act.wait_ge(m["lg"], b.value("lg", 1))
                    nc.scalar.activation(eg[s][:], lg[s][:], ACT.Exp).then_inc(m["eg"], 1)
                if name == "ev8":
                    act.wait_ge(*b.full("pv8", k))
                    nc.scalar.activation(oU[s][:, k, :], pv8[:, 0:SEQ], ACT.Copy).then_inc(ring_done["pn"], 1)
                if ring != "st":
                    return
                act.wait_ge(*b.full(name, k))
                ps = b.slot(name, k)
                done = ring_done["st"]
                if name == "qp":
                    heads = ps[0:CD].rearrange("p (h n) -> p h n", h=4)
                    nc.scalar.activation(qAb[:, 4 * k:4 * k + 4, :], heads, ACT.Copy)
                    nc.scalar.activation(qA[0:CD, 4 * k:4 * k + 4, :], heads, ACT.Copy).then_inc(done, 1)
                    if k == 1:
                        act.wait_ge(m["ctx"], b.value("ctx", 16))
                        nc.scalar.activation(cTb[:], cT["X"][0:CD, :], ACT.Copy).then_inc(m["ctb"], 1)
                elif name == "vp":
                    nc.scalar.activation(vX[:, 2 * k:2 * k + 2, :], ps.rearrange("p (h n) -> p h n", h=2),
                                         ACT.Copy).then_inc(done, 1)
                elif name == "e":
                    if k >= SLOTS[s]:
                        act.wait_ge(m["pv"], b.value("pv", (k - SLOTS[s]) // 2 + 1))
                    nc.scalar.activation(prob[s][k % SLOTS[s]][:], ps, ACT.Exp, scale=float(XD) ** -0.5).then_inc(done, 1)
                elif name in ("qk", "kk"):
                    where = {"F": [(0, 0, SEQ, 0), (SEQ, 512, SEQ, 1)], "K": [(0, 0, KV, 1)]}[s]
                    for to, at, n, j in where:
                        bias = bq8["B" if s == "K" else s][:, j:j + 1]
                        nc.scalar.activation(parts[s][:, 0, to:to + n], ps[:, at:at + n], ACT.Identity, bias=bias)
                        last = nc.scalar.activation(qk[s][:, to:to + n], ps[:, at:at + n], ACT.Identity, bias=bias)
                    last.then_inc(done, 1)
                elif name == "e8":
                    if k >= SLOTS[s]:
                        act.wait_ge(*b.full("pv8", (k - SLOTS[s]) // NC[s]))
                    nc.scalar.activation(prob[s][k % SLOTS[s]][:], ps, ACT.Exp, scale=float(D8) ** -0.5).then_inc(done, 1)
            run(act, step)
        @block.vector
        def _(dve):
            def step(b, name, k, ring):
                s, m = b.s, S[b.s]
                calls = link_of[b.stage]
                if (name, k) == FIRST[b.stage]:
                    calls[0] = LINKS_BEFORE["dve"].get(b.stage, 0)

                def link(ins):
                    calls[0] += 1
                    ins.then_inc(m["vch"], 1)
                    dve.wait_ge(m["vch"], b.value("vch", calls[0]))

                if name == "ls":
                    src = source[s, k]
                    if s == "X":
                        dve.wait_ge(m["xin"], b.value("xin", 16))
                    elif s == "F":
                        dve.wait_ge(*b.beside("x").done("out"))
                    elif s == "B":
                        dve.wait_ge(S["F"]["xm"], (b.batch + 1) * COUNTS["F"]["xm"])
                    else:
                        dve.wait_ge(*b.before("sm"))
                    for t in range(QT):
                        last = nc.vector.bn_stats(st6[s][:, t, :], src[:, t, :])
                    link(last)
                    apart(dve)
                    for t in range(QT):
                        last = nc.vector.bn_aggr(mv[s][:, t, :], st6[s][:, t, :])
                    last.then_inc(m["mv"], 1)
                if name == "ln":
                    src = source[s, k]
                    dve.wait_ge(m["rstd"], b.value("rstd", k + 1))
                    for t in range(QT):
                        last = nc.vector.tensor_scalar(xh[s][:, t, :], src[:, t, :], mv[s][:, t, 0:1], rstd[s][:, t:t + 1],
                                                       ALU.subtract, ALU.mult)
                    last.then_inc(m["xh"], 1)
                if name == "nx":
                    dve.wait_ge(m["pv"], b.value("pv", k + 1))
                    link(nc.vector.reciprocal(rden[:], pvx[:, SEQ:2 * SEQ]))
                    nc.vector.tensor_tensor(oTX[:, k, :], pvx[:, 0:SEQ], rden[:], ALU.mult).then_inc(m["norm"], 1)
                if name == "sp":
                    dve.wait_ge(*b.done("kk" if s == "K" else "qk"))
                    link(nc.vector.tensor_tensor(qk[s][:], qk[s][:], parts[s][:, 0, :], ALU.subtract))
                    link(nc.vector.tensor_copy(parts[s][:, 1, :], qk[s][:]))
                    nc.vector.tensor_tensor(parts[s][:, 2, :], qk[s][:], parts[s][:, 1, :], ALU.subtract)\
                        .then_inc(m["split"], 1)
                if name == "gx":
                    dve.wait_ge(m["eg"], b.value("eg", 1))
                    link(nc.vector.tensor_reduce(sg[s][:], eg[s][:], AX.X, ALU.add))
                    link(nc.vector.reciprocal(sg[s][:], sg[s][:]))
                    link(nc.vector.tensor_tensor(pr[s][:], eg[s][:], sg[s][:].rearrange("p (t o) -> p t o", o=1)
                                                 .broadcast_to([P, QT, NE]), ALU.mult))
                    apart(dve)
                    for t in range(QT):
                        last = nc.vector.max(top[s][:, t, :], pr[s][:, t, :])
                    link(last)
                    apart(dve)
                    for t in range(QT):
                        last = nc.vector.max_index(tix[s][:, t, :], top[s][:, t, :], pr[s][:, t, :])
                    link(last)
                    link(nc.vector.tensor_copy(tif[s][:], tix[s][:]))
                    for t in range(QT):
                        for wt_, j in ((w0, 0), (w1, 1)):
                            last = nc.vector.scalar_tensor_tensor(out=wt_[s][:, t, :], in0=iota[:], scalar=tif[s][:, t, j:j + 1],
                                                                  in1=pr[s][:, t, :], op0=ALU.is_equal, op1=ALU.mult)
                    link(last)
                    if s == "F":
                        nc.vector.tensor_tensor(w[s][:], w0[s][:], w1[s][:], ALU.add).then_inc(m["w"], 1)
                    else:
                        link(nc.vector.tensor_tensor(w[s][:], w0[s][:], w1[s][:], ALU.add))
                        link(nc.vector.tensor_reduce(ts[:], w[s][:], AX.X, ALU.add))
                        link(nc.vector.tensor_scalar(ts[:], ts[:], 1e-6, None, ALU.add))
                        link(nc.vector.reciprocal(ts[:], ts[:]))
                        link(nc.vector.tensor_tensor(w[s][:], w[s][:], ts[:].rearrange("p (t o) -> p t o", o=1)
                                                     .broadcast_to([P, QT, NE]), ALU.mult))
                        link(nc.vector.tensor_tensor(wp[:], w[s][:], pr[s][:], ALU.mult))
                        nc.vector.tensor_reduce(cb[:], wp[:], AX.X, ALU.add).then_inc(m["w"], 1)
                if ring != "sm":
                    return
                dve.wait_ge(*b.full(name, k))
                ps = b.slot(name, k)
                done = ring_done["sm"]
                tiles = ps[:, 0:QT * P].rearrange("p (t n) -> p t n", t=QT)
                if name == "ln":
                    nc.vector.tensor_copy(xT[s][:], ps[:, 0:SEQ]).then_inc(done, 1)
                elif name == "qk":
                    nc.vector.tensor_scalar(parts[s][:, 0, :], ps[:, 0:SEQ], bq8[s][:, 0:1], None, ALU.add)
                    nc.vector.tensor_scalar(qk[s][:], ps[:, 0:SEQ], bq8[s][:, 0:1], None, ALU.add).then_inc(done, 1)
                elif name == "mx":
                    h, t = divmod(k, QT)
                    nc.vector.tensor_reduce(mxA[:, t, h:h + 1], ps, AX.X, ALU.max, negate=True).then_inc(done, 1)
                elif name == "mT":
                    nc.vector.tensor_copy(mrow[:], ps[0:XH, 0:SEQ]).then_inc(done, 1)
                elif name in ("out", "out8"):
                    dve.wait_ge(m["xb"], b.value("xb", 1))
                    dve.wait_ge(S["F" if s == "X" else "C"]["fin"], b.batch)
                    nc.vector.scalar_tensor_tensor(out=x1["F" if s == "X" else "B"][:], in0=tiles,
                                                   scalar=gates[:, 0:1] if s == "X" else gates[:, 1:2], in1=xb[s][:],
                                                   op0=ALU.mult, op1=ALU.add).then_inc(done, 1)
                elif name == "wb":
                    dve.wait_ge(m["fin"], b.value("fin", 1))
                    nc.vector.scalar_tensor_tensor(out=fin[s][:], in0=tiles, scalar=gates[:, 2:3], in1=fin[s][:],
                                                   op0=ALU.mult, op1=ALU.add).then_inc(done, 1)
                elif name == "oT":
                    heads = ps.rearrange("p (h n) -> p h n", h=H8)
                    link(nc.vector.reciprocal(rr[s][:, k, :], heads[:, :, D8]))
                    nc.vector.tensor_tensor(att[s][:, k, :].rearrange("p (h d) -> p h d", h=H8), heads[:, :, 0:D8],
                                            rr[s][:, k, :].rearrange("p (h o) -> p h o", o=1).broadcast_to([P, H8, D8]),
                                            ALU.mult).then_inc(done, 1)
                    if s == "F":
                        dve.wait_ge(*b.done("oT", k))
                        if k == 0:
                            dve.wait_ge(S["B"]["xb"], b.batch)
                        nc.vector.scalar_tensor_tensor(out=xmid[:, k, :], in0=att[s][:, k, :], scalar=gates[:, 2:3],
                                                       in1=fin["F"][:, k, :], op0=ALU.mult, op1=ALU.add).then_inc(m["xm"], 1)
                elif name == "aT":
                    nc.vector.tensor_copy(attT[:], ps[:, 0:SEQ]).then_inc(done, 1)
                elif name in ("v8", "vv"):
                    to = "F" if s == "F" else "B"
                    nc.vector.tensor_tensor(
                        v8[to][:, 2 * k:2 * k + 2, :, 0:D8],
                        ps[:, 0:2 * P].rearrange("p (c h d) -> p c h d", c=2, h=H8),
                        bv8[to][:].rearrange("p (o h d) -> p o h d", o=1, h=H8).broadcast_to([P, 2, H8, D8]),
                        ALU.add).then_inc(done, 1)
                elif name == "gate":
                    psl = ps[:, 0:QT * NE].rearrange("p (t e) -> p t e", t=QT)
                    if s == "F":
                        nc.vector.tensor_tensor(lg[s][:], psl, bg[:].rearrange("p (o e) -> p o e", o=1)
                                                .broadcast_to([P, QT, NE]), ALU.add).then_inc(done, 1)
                    else:
                        nc.vector.tensor_copy(lg[s][:], psl).then_inc(done, 1)
                    dve.wait_ge(*b.done(name, k))
                    link(nc.vector.tensor_reduce(nm[s][:], lg[s][:], AX.X, ALU.max, negate=True))
                    nmb = nm[s][:].rearrange("p (t o) -> p t o", o=1).broadcast_to([P, QT, NE])
                    nc.vector.tensor_tensor(lg[s][:], lg[s][:], nmb, ALU.add).then_inc(m["lg"], 1)
                elif name == "wT":
                    nc.vector.tensor_copy(wT[:], ps[0:NE, 0:SEQ]).then_inc(done, 1)
                elif name == "moe":
                    t, f = divmod(k, 2)
                    dve.wait_ge(m["w"], b.value("w", 1))
                    dve.wait_ge(m["used"], b.value("used", k - 1))
                    nc.vector.tensor_tensor(
                        prod[s][k % 2][:].rearrange("p (e n) -> p e n", e=4), ps.rearrange("p (e n) -> p e n", e=4),
                        w[s][:, t, 4 * f:4 * f + 4].rearrange("p (e o) -> p e o", o=1).broadcast_to([P, 4, P]),
                        ALU.mult).then_inc(done, 1)
                elif name == "mx8":
                    if s == "F":
                        nc.vector.tensor_reduce(mx8[s][:, :, k], ps.rearrange("p (t n) -> p t n", t=QT), AX.X, ALU.max,
                                                negate=True).then_inc(done, 1)
                    else:
                        h, t = 2 * (k // 4) + k % 2, k // 2 % 2
                        nc.vector.tensor_reduce(mx8[s][:, t, h:h + 1], ps, AX.X, ALU.max, negate=True).then_inc(done, 1)
                elif name == "mT8":
                    link(nc.vector.tensor_copy(m2[s][:, 0, :], ps[0:H8, 0:SEQ]))
                    nc.vector.tensor_tensor(m2[s][:, 1, :], ps[0:H8, 0:SEQ], m2[s][:, 0, :], ALU.subtract)\
                        .then_inc(done, 1)

            link_of = {s: [0] for s in LAG}
            run(dve, step)
            assert all(link_of[s][0] == COUNTS[s.upper()]["vch"] for s in "xfKbc"), link_of

        @block.gpsimd
        def _(pool):
            for (s, n), credit in CREDIT.items():
                pool.sem_inc(S[s][n], credit)
            for tile in (cT["X"], ones, cT["K"], k8["F"], k8["B"], v8["F"], v8["B"]):
                pool.memset(tile[:], 1.0).then_inc(c_set, 1)
            pool.memset(nhalf[:], -0.5)
            pool.wait_ge(w_first, W_FIRST)
            pool.wait_ge(tanh_done, 1)
            for n, s in enumerate("XB"):
                pool.tensor_scalar(bo[s][:], bo[s][:], gates[:, n:n + 1], None, ALU.mult).then_inc(bias_done, 1)
            pool.wait_ge(bias_done, 2)

            def step(b, name, k, ring):
                s, m = b.s, S[b.s]
                calls = link_of[b.stage]
                if (name, k) == FIRST[b.stage]:
                    calls[0] = LINKS_BEFORE["pool"].get(b.stage, 0)

                def link(ins):
                    calls[0] += 1
                    ins.then_inc(m["pch"], 1)
                    pool.wait_ge(m["pch"], b.value("pch", calls[0]))

                if name == "ls":
                    pool.wait_ge(m["mv"], b.value("mv", k + 1))
                    apart(pool)
                    link(pool.tensor_scalar(ve[s][:], mv[s][:, :, 1], EPS, None, ALU.add))
                    pool.tensor_tensor(rstd[s][:], ve[s][:], nhalf[:], ALU.pow).then_inc(m["rstd"], 1)
                    if s in "XB":
                        pool.tensor_tensor(xb[s][:], source[s, 0][:], bo[s][:].rearrange("p (o n) -> p o n", o=1)
                                           .broadcast_to([P, QT, P]), ALU.add).then_inc(m["xb"], 1)
                elif name == "e":
                    pool.wait_ge(*b.done("e", k))
                    if k >= 4:
                        pool.wait_ge(m["pv"], b.value("pv", (k - 4) // 2 + 1))
                    pool.wait_ge(m["psum"], b.value("psum", k))
                    p = prob[s][k % SLOTS[s]]
                    link(pool.tensor_tensor(half[:], p[:, 0:2 * SEQ], p[:, 2 * SEQ:], ALU.add))
                    pool.tensor_tensor(psum_k[k % 4][:], half[:, 0:SEQ], half[:, SEQ:], ALU.add).then_inc(m["psum"], 1)
                elif name == "moe":
                    t, f = divmod(k, 2)
                    pr_ = prod[s][k % 2]
                    pool.wait_ge(*b.done("moe", k))
                    link(pool.tensor_tensor(pr_[:, 0:2 * P], pr_[:, 0:2 * P], pr_[:, 2 * P:], ALU.add))
                    if f == 0:
                        pool.tensor_tensor(acc[s][:, t, :], pr_[:, 0:P], pr_[:, P:2 * P], ALU.add).then_inc(m["used"], 1)
                        return
                    link(pool.tensor_tensor(pr_[:, 0:P], pr_[:, 0:P], pr_[:, P:2 * P], ALU.add))
                    pool.tensor_tensor(acc[s][:, t, :], acc[s][:, t, :], pr_[:, 0:P], ALU.add).then_inc(m["used"], 1)
                    if k < 3:
                        return
                    pool.wait_ge(m["used"], b.value("used", 4))
                    pool.wait_ge(m["w"], b.value("w", 1))
                    apart(pool)
                    if s == "F":
                        link(pool.tensor_scalar(acc[s][:], acc[s][:], gates[:, 2:3], None, ALU.mult))
                        pool.wait_ge(m["xm"], b.value("xm", 0))
                    else:
                        for t in range(QT):
                            last = pool.tensor_scalar(acc[s][:, t, :], acc[s][:, t, :], cb[:, t:t + 1], gates[:, 3:4],
                                                      ALU.add, ALU.mult)
                        link(last)
                        pool.wait_ge(m["out"], b.value("out", 0))
                    pool.tensor_tensor(fin[s][:], acc[s][:], x1[s][:], ALU.add).then_inc(m["fin"], 1)
            link_of = {s: [0] for s in LAG}
            run(pool, step)
            assert all(link_of[s][0] == COUNTS[s.upper()]["pch"] for s in "xFbc"), link_of


def kernel(**inputs):
    import concourse.bacc as bacc
    from concourse.bass_utils import run_bass_kernel_spmd

    g = {k: np.asarray(v) for k, v in inputs.items()}

    def dh(m):
        return m.reshape(m.shape[:-1] + (H8, D8)).swapaxes(-1, -2).reshape(m.shape)

    wqkv, bqkv = g["L0_ffn_W_qkv"], g["L0_ffn_b_qkv"]
    wkv, bkv = g["L1_xattn_Wkv"], g["L1_xattn_bkv"]
    arrays = {
        "x": g["x"], "ctxT": g["ctx_768"].transpose(0, 2, 1), "g_xattn": g["g_xattn"], "g_ffn": g["g_ffn"],
        "ident": np.eye(P, dtype=np.float32),
        "iota": np.tile(np.arange(NE, dtype=np.float32), (P, 1)),
        "wqT": g["L0_xattn_Wq"].reshape(P, XH, XD).transpose(2, 1, 0),
        "wkT": g["L0_xattn_Wk"].reshape(CD, XH, XD).transpose(2, 1, 0),
        "wvx": g["L0_xattn_Wv"], "wox": g["L0_xattn_Wo"].reshape(XH // 2, P, P).transpose(1, 0, 2),
        "boX": g["L0_xattn_bo"], "boB": g["L1_xattn_bo"],
        "wq8F": dh(wqkv[:, :P]), "wk8F": dh(wqkv[:, P:2 * P]), "wv8F": wqkv[:, 2 * P:],
        "bq8F": dh(bqkv[:2 * P].reshape(2, P)).T, "bv8F": bqkv[2 * P:],
        "wq8B": dh(g["L1_xattn_Wq"]), "wk8B": dh(wkv[:, :P]), "wv8B": wkv[:, P:],
        "bq8B": np.stack([dh(g["L1_xattn_bq"]), dh(bkv[:P])], axis=1), "bv8B": bkv[P:],
        "wo8": g["L1_xattn_Wo"],
        "wgF": g["L0_ffn_W_gate"], "wgB": g["L1_ffn_router_w"].T, "bg": g["L0_ffn_b_gate"],
        "weF": g["L0_ffn_W_experts"], "weB": g["L1_ffn_expert_weights"], "be": g["L0_ffn_b_experts"],
    }
    arrays = {"in_" + k: np.ascontiguousarray(v) for k, v in arrays.items()}
    nc = bacc.Bacc("TRN2", target_bir_lowering=False, num_devices=1)
    handles = {k[3:]: nc.dram_tensor(k, v.shape, mybir.dt.from_np(v.dtype), kind="ExternalInput").ap()
               for k, v in arrays.items()}
    out = nc.dram_tensor("out", (BATCH, SEQ, P), F32, kind="ExternalOutput").ap()
    build(nc, handles, out)
    r = run_bass_kernel_spmd(nc, [arrays], core_ids=[0])
    return r.results[0]["out"]
```
